# Optimizing a Trainium2 kernel written in Bass

```python
import numpy as np
import jax
import jax.numpy as jnp

def _softmax(x, axis=-1):
    return jax.nn.softmax(x, axis=axis)

def _gelu(x):
    return jax.nn.gelu(x, approximate=True)

def _silu(x):
    return jax.nn.silu(x)

def _sigmoid(x):
    return jax.nn.sigmoid(x)

def _layernorm(x, axis=-1, eps=1e-05):
    m = jnp.mean(x, axis=axis, keepdims=True)
    v = jnp.var(x, axis=axis, keepdims=True)
    return (x - m) / jnp.sqrt(v + eps)

def _scatter_add(tgt, idx, src, axis=0):
    return tgt.at[idx].add(src)

def _segment_sum(src, seg, n):
    return jax.ops.segment_sum(src, seg, n)
kernel_name = 'mk_adj_preln_d4_adj_r2_964129'

def setup_inputs(seed: int=0):
    np.random.seed(seed)
    _w = jnp.asarray

    def _rec_inputs():
        import jax
        import jax.numpy as jnp
        _gk = jax.random.key(seed)
        x = -0.0005207 + 1.001 * jax.random.normal(jax.random.fold_in(_gk, 1), (8, 1024, 128), jnp.float32)
        _a = jax.random.bernoulli(jax.random.fold_in(_gk, 2), 0.015625, (1024, 1024))
        _a = jnp.logical_or(_a, jnp.swapaxes(_a, -1, -2))
        _a = jnp.logical_or(_a, jnp.eye(1024, dtype=bool))
        adj = _a.astype(jnp.int32)
        return (x, adj)
    x, adj = _rec_inputs()

    def _L0_gnn_setup():
        import jax, jax.numpy as jnp
        import numpy as np
        import math
        CHUNK = 128
        NUM_HEADS = 4
        EPS = 1e-05
        key = jax.random.key(seed)
        ks = jax.random.split(key, 12)
        B, N, F = (4, 1024, 128)
        x = jax.random.normal(ks[0], (B, N, F), dtype=jnp.float32)
        adj_matrix = jax.random.randint(ks[1], (N, N), 0, 2, dtype=jnp.int32)
        s = 1.0 / math.sqrt(F)
        Wq = jax.random.normal(ks[2], (F, F), dtype=jnp.float32) * s
        bq = jnp.zeros((F,), dtype=jnp.float32)
        Wk = jax.random.normal(ks[3], (F, F), dtype=jnp.float32) * s
        bk = jnp.zeros((F,), dtype=jnp.float32)
        Wv = jax.random.normal(ks[4], (F, F), dtype=jnp.float32) * s
        bv = jnp.zeros((F,), dtype=jnp.float32)
        Wo = jax.random.normal(ks[5], (F, F), dtype=jnp.float32) * s
        bo = jnp.zeros((F,), dtype=jnp.float32)
        gamma = jnp.ones((F,), dtype=jnp.float32)
        beta = jnp.zeros((F,), dtype=jnp.float32)
        return {'x': x, 'adj_matrix': adj_matrix, 'Wq': Wq, 'bq': bq, 'Wk': Wk, 'bk': bk, 'Wv': Wv, 'bv': bv, 'Wo': Wo, 'bo': bo, 'gamma': gamma, 'beta': beta}
    _L0_gnn_all = _L0_gnn_setup()
    _L0_gnn_in = {k: v for k, v in _L0_gnn_all.items() if k in ('Wq', 'bq', 'Wk', 'bk', 'Wv', 'bv', 'Wo', 'bo', 'gamma', 'beta')}
    del _L0_gnn_all

    def _L1_gnn_setup():
        import jax, jax.numpy as jnp
        import numpy as np
        ALPHA = 0.2
        MASK_VAL = -9000000000000000.0
        key = jax.random.key(seed)
        k1, k2, k3, k4 = jax.random.split(key, 4)
        B, N, F = (8, 512, 128)
        H, OUT = (4, 128)
        hs = OUT // H
        x = jax.random.normal(k1, (B, N, F), dtype=jnp.float32)
        adj = jax.random.randint(k2, (N, N), 0, 2, dtype=jnp.int32)
        wb = float(np.sqrt(6.0 / (F + hs)))
        ab = float(np.sqrt(6.0 / (H + 2 * hs)))
        W = jax.random.uniform(k3, (H, F, hs), dtype=jnp.float32, minval=-wb, maxval=wb)
        a = jax.random.uniform(k4, (H, 2 * hs), dtype=jnp.float32, minval=-ab, maxval=ab)
        return {'x': x, 'adj': adj, 'W': W, 'a': a}
    _L1_gnn_all = _L1_gnn_setup()
    _L1_gnn_in = {k: v for k, v in _L1_gnn_all.items() if k in ('W', 'a')}
    del _L1_gnn_all

    def _L2_gnn_setup():
        import jax, jax.numpy as jnp
        import numpy as np
        ALPHA = 0.2
        EPS = 1e-06
        key = jax.random.key(seed)
        ks = jax.random.split(key, 8)
        B, N, D, H = (2, 1024, 128, 8)
        dh = D // H
        x = jax.random.normal(ks[0], (B, N, D), dtype=jnp.float32)
        adj = jax.random.randint(ks[1], (N, N), 0, 2, dtype=jnp.int32)
        adj = jnp.maximum(adj, jnp.eye(N, dtype=jnp.int32))
        p = jax.random.uniform(ks[2], (B, N, N), dtype=jnp.float32)
        prior = p / jnp.sum(p, axis=-1, keepdims=True)
        W = jax.random.normal(ks[3], (H, D, dh), dtype=jnp.float32) * (1.0 / np.sqrt(D))
        a_src = jax.random.normal(ks[4], (H, dh), dtype=jnp.float32) * (1.0 / np.sqrt(dh))
        a_dst = jax.random.normal(ks[5], (H, dh), dtype=jnp.float32) * (1.0 / np.sqrt(dh))
        beta_tilde = jnp.ones((), dtype=jnp.float32)
        W_out = jax.random.normal(ks[6], (D, D), dtype=jnp.float32) * (1.0 / np.sqrt(D))
        return {'x': x, 'adj': adj, 'prior': prior, 'W': W, 'a_src': a_src, 'a_dst': a_dst, 'beta_tilde': beta_tilde, 'W_out': W_out}
    _L2_gnn_all = _L2_gnn_setup()
    _L2_gnn_in = {k: v for k, v in _L2_gnn_all.items() if k in ('W', 'a_src', 'a_dst', 'beta_tilde', 'W_out')}
    del _L2_gnn_all

    def _L3_gnn_setup():
        import jax, jax.numpy as jnp
        import numpy as np
        ALPHA = 0.2
        NEG_INF = -1000000000000.0
        key = jax.random.key(seed)
        k1, k2, k3, k4, k5 = jax.random.split(key, 5)
        B, N, C_in, C_out = (8, 1024, 128, 128)
        inp = jax.random.normal(k1, (B, N, C_in), dtype=jnp.float32)
        adj = jax.random.randint(k2, (N, N), 0, 2, dtype=jnp.int32)
        limit = 1.414 * np.sqrt(6.0 / (C_in + C_out))
        W1 = jax.random.uniform(k3, (C_in, C_out), jnp.float32, -limit, limit)
        W2 = jax.random.uniform(k4, (C_in, C_out), jnp.float32, -limit, limit)
        W3 = jax.random.uniform(k5, (C_in, C_out), jnp.float32, -limit, limit)
        return {'inp': inp, 'adj': adj, 'W1': W1, 'W2': W2, 'W3': W3}
    _L3_gnn_all = _L3_gnn_setup()
    _L3_gnn_in = {k: v for k, v in _L3_gnn_all.items() if k in ('W1', 'W2', 'W3')}
    del _L3_gnn_all
    return {'x': x, 'adj': adj, 'L0_gnn_Wq': _L0_gnn_in['Wq'], 'L0_gnn_bq': _L0_gnn_in['bq'], 'L0_gnn_Wk': _L0_gnn_in['Wk'], 'L0_gnn_bk': _L0_gnn_in['bk'], 'L0_gnn_Wv': _L0_gnn_in['Wv'], 'L0_gnn_bv': _L0_gnn_in['bv'], 'L0_gnn_Wo': _L0_gnn_in['Wo'], 'L0_gnn_bo': _L0_gnn_in['bo'], 'L0_gnn_gamma': _L0_gnn_in['gamma'], 'L0_gnn_beta': _L0_gnn_in['beta'], 'L1_gnn_W': _L1_gnn_in['W'], 'L1_gnn_a': _L1_gnn_in['a'], 'L2_gnn_W': _L2_gnn_in['W'], 'L2_gnn_a_src': _L2_gnn_in['a_src'], 'L2_gnn_a_dst': _L2_gnn_in['a_dst'], 'L2_gnn_beta_tilde': _L2_gnn_in['beta_tilde'], 'L2_gnn_W_out': _L2_gnn_in['W_out'], 'L3_gnn_W1': _L3_gnn_in['W1'], 'L3_gnn_W2': _L3_gnn_in['W2'], 'L3_gnn_W3': _L3_gnn_in['W3']}

def reference(x, adj, L0_gnn_Wq, L0_gnn_bq, L0_gnn_Wk, L0_gnn_bk, L0_gnn_Wv, L0_gnn_bv, L0_gnn_Wo, L0_gnn_bo, L0_gnn_gamma, L0_gnn_beta, L1_gnn_W, L1_gnn_a, L2_gnn_W, L2_gnn_a_src, L2_gnn_a_dst, L2_gnn_beta_tilde, L2_gnn_W_out, L3_gnn_W1, L3_gnn_W2, L3_gnn_W3):
    import jax
    import jax.numpy as jnp

    def _L0_gnn_ref(x, adj_matrix, Wq, bq, Wk, bk, Wv, bv, Wo, bo, gamma, beta):
        import jax, jax.numpy as jnp
        import numpy as np
        import math
        CHUNK = 128
        NUM_HEADS = 4
        EPS = 1e-05
        B, N, Fin = x.shape
        H = NUM_HEADS
        Dout = Wq.shape[0]
        Dh = Dout // H
        Nc = N // CHUNK
        q = (x @ Wq.T + bq).reshape(B, N, H, Dh).transpose(0, 2, 1, 3)
        k = (x @ Wk.T + bk).reshape(B, N, H, Dh).transpose(0, 2, 1, 3)
        v = (x @ Wv.T + bv).reshape(B, N, H, Dh).transpose(0, 2, 1, 3)
        kc = k.reshape(B, H, Nc, CHUNK, Dh)
        vc = v.reshape(B, H, Nc, CHUNK, Dh)
        scores = jnp.einsum('bhnd,bhjcd->bhnjc', q, kc) / jnp.sqrt(jnp.asarray(Dh, dtype=q.dtype))
        scores = jnp.clip(scores, -10.0, 10.0)
        mask = adj_matrix.reshape(N, Nc, CHUNK)[None, None]
        scores = jnp.where(mask == 0, jnp.asarray(-10.0, scores.dtype), scores)
        attn = jax.nn.softmax(scores, axis=-1)
        ctx = jnp.einsum('bhnjc,bhjcd->bhnd', attn, vc)
        ctx = ctx.transpose(0, 2, 1, 3).reshape(B, N, Dout)
        out = ctx @ Wo.T + bo
        out = out + x
        mu = jnp.mean(out, axis=-1, keepdims=True)
        var = jnp.mean(jnp.square(out - mu), axis=-1, keepdims=True)
        out = (out - mu) * jax.lax.rsqrt(var + EPS) * gamma + beta
        return out

    def _L1_gnn_ref(x, adj, W, a):
        import jax, jax.numpy as jnp
        import numpy as np
        ALPHA = 0.2
        MASK_VAL = -9000000000000000.0
        B, N, _ = x.shape
        H, _, hs = W.shape
        Wh = jnp.einsum('bnf,hfd->bhnd', x, W)
        a1, a2 = (a[:, :hs], a[:, hs:])
        ei = jnp.einsum('bhnd,hd->bhn', Wh, a1)
        ej = jnp.einsum('bhnd,hd->bhn', Wh, a2)
        e = ei[:, :, :, None] + ej[:, :, None, :]
        e = jnp.where(e > 0, e, ALPHA * e)
        e = jnp.where(adj[None, None] > 0, e, MASK_VAL)
        att = jax.nn.softmax(e, axis=-1)
        h = jnp.einsum('bhij,bhjd->bhid', att, Wh)
        h = h.transpose(0, 2, 1, 3).reshape(B, N, H * hs)
        return jax.nn.elu(h)

    def _L2_gnn_ref(x, adj, prior, W, a_src, a_dst, beta_tilde, W_out):
        import jax, jax.numpy as jnp
        import numpy as np
        ALPHA = 0.2
        EPS = 1e-06
        B, N, D = x.shape
        x_proj = jnp.einsum('bnd,hdf->bhnf', x, W)
        e_src = jnp.einsum('bhnf,hf->bhn', x_proj, a_src)
        e_dst = jnp.einsum('bhnf,hf->bhn', x_proj, a_dst)
        e = jax.nn.leaky_relu(e_src[..., :, None] + e_dst[..., None, :], ALPHA)
        beta = jax.nn.softplus(beta_tilde)
        e = e + (beta * jnp.log(prior + EPS))[:, None, :, :]
        neg_inf = jnp.finfo(e.dtype).min
        e = jnp.where(adj[None, None, :, :] > 0, e, neg_inf)
        attn = jax.nn.softmax(e, axis=-1)
        h = jnp.einsum('bhij,bhjf->bhif', attn, x_proj)
        h = h.transpose(0, 2, 1, 3).reshape(B, N, D)
        return h @ W_out.T

    def _L3_gnn_ref(inp, adj, W1, W2, W3):
        import jax, jax.numpy as jnp
        import numpy as np
        ALPHA = 0.2
        NEG_INF = -1000000000000.0
        h1 = jnp.einsum('bnc,cd->bnd', inp, W1)
        h2 = jnp.einsum('bnc,cd->bnd', inp, W2)
        h3 = jnp.einsum('bnc,cd->bnd', inp, W3)
        e = jnp.einsum('bnd,bmd->bnm', h1, h2)
        e = jax.nn.leaky_relu(e, ALPHA)
        e = jnp.where(adj[None, :, :] > 0, e, NEG_INF)
        attention = jax.nn.softmax(e, axis=-1)
        h_prime = jnp.einsum('bnm,bmd->bnd', attention, h3)
        return jax.nn.relu(h_prime)
    h = jnp.maximum(_layernorm(x, axis=-1), 0.0)
    x = x + _L0_gnn_ref(h, adj, L0_gnn_Wq, L0_gnn_bq, L0_gnn_Wk, L0_gnn_bk, L0_gnn_Wv, L0_gnn_bv, L0_gnn_Wo, L0_gnn_bo, L0_gnn_gamma, L0_gnn_beta)
    h = jnp.maximum(_layernorm(x, axis=-1), 0.0)
    x = x + _L1_gnn_ref(h, adj, L1_gnn_W, L1_gnn_a)
    h = jnp.maximum(_layernorm(x, axis=-1), 0.0)
    x = x + _L2_gnn_ref(h, adj, adj[None], L2_gnn_W, L2_gnn_a_src, L2_gnn_a_dst, L2_gnn_beta_tilde, L2_gnn_W_out)
    h = jnp.maximum(_layernorm(x, axis=-1), 0.0)
    x = x + _L3_gnn_ref(h, adj, L3_gnn_W1, L3_gnn_W2, L3_gnn_W3)
    return x

_drawn_inputs = setup_inputs


def setup_inputs(seed=0):
    import zlib

    import numpy as np

    out = dict(_drawn_inputs(seed))
    spreads = {'L0_gnn_bq': (0.0, 0.8),
     'L0_gnn_bk': (0.0, 2.0),
     'L0_gnn_bv': (0.0, 0.1),
     'L0_gnn_bo': (0.0, 0.354),
     'L0_gnn_gamma': (1.0, 0.2),
     'L0_gnn_beta': (0.0, 0.1)}
    factors = {'L2_gnn_a_src': 2.837}
    for name, (base, spread) in spreads.items():
        noise = np.random.default_rng([zlib.crc32(name.encode()), seed]).standard_normal(out[name].shape)
        drawn = base * np.exp(spread * noise) if base else spread * noise
        out[name] = jnp.asarray(drawn.astype(out[name].dtype))
    for name, factor in factors.items():
        out[name] = (out[name] * factor).astype(out[name].dtype)
    return out
```

```python
from contextlib import ExitStack

import concourse.bass as bass
from concourse import mybir

F32 = mybir.dt.float32
F32R = mybir.dt.float32r
BF16 = mybir.dt.bfloat16
I32 = mybir.dt.int32
ALU = mybir.AluOpType
ACT = mybir.ActivationFunctionType
AX = mybir.AxisListType
RMAX = bass.bass_isa.ReduceOp.max

P = 128
B, N, F = 8, 1024, 128
T = N // P
HALF = 512
EPS = 1e-5
CLIP_LO, CLIP_HI = 4.5399929762484854e-05, 22026.465794806718
STEEP = 2.0 ** 60
NEG = -1.0e30


class Core:

    def __init__(self, nc, ctx):
        self.nc = nc
        self.ctx = ctx
        sb = self.sb
        self.x = sb("x", [P, B, T, F], F32)
        self.h = sb("h", [P, 2, T, F], F32)
        self.h_t = sb("h_t", [P, N], F32)
        self.ident = sb("ident", [P, P], F32)
        self.ones = sb("ones", [P, 1], F32)
        self.mhalf = sb("mhalf", [P, T], F32)
        self.stats = sb("stats", [P, T, 6], F32)
        self.moments = sb("moments", [P, T, 2], F32)
        self.var_eps = sb("var_eps", [P, T], F32)
        self.rstd = sb("rstd", [P, T], F32)
        self.passed = self.sem("passed")
        self.norm_sems = [self.sem(name) for name in ("stats_done", "moments_done", "var_done", "rstd_done",
                                                      "scaled", "h_ready", "h_turned", "h_t_ready")]

    def sb(self, name, shape, dt, ctx=None):
        return (ctx or self.ctx).enter_context(self.nc.sbuf_tensor(name, shape, dt))

    def ps(self, name, shape, ctx):
        return ctx.enter_context(self.nc.psum_tensor(name, shape, F32))

    def sem(self, name):
        return self.ctx.enter_context(self.nc.semaphore(name))


class Norm:

    def __init__(self, c, layer, aux):
        self.c, self.aux, self.layer = c, aux, layer
        (self.stats_done, self.moments_done, self.var_done, self.rstd_done, self.scaled, self.h_ready,
         self.h_turned, self.h_t_ready) = c.norm_sems

    def upto(self, n):
        return n + B * self.layer + 1

    def dve_stats(self, eng, n):
        c = self.c
        for t in range(T):
            ins = eng.bn_stats(c.stats[:, t, :], c.x[:, n, t, :])
        ins.then_inc(self.stats_done, 1)

    def dve_moments(self, eng, n):
        c = self.c
        wait_apart(self.c, eng, self.stats_done, self.upto(n))
        for t in range(T):
            ins = eng.bn_aggr(c.moments[:, t, :], c.stats[:, t, :])
        ins.then_inc(self.moments_done, 1)
        eng.wait_ge(self.moments_done, self.upto(n))
        eng.tensor_scalar(c.var_eps[:, :], c.moments[:, :, 1], EPS, None, ALU.add).then_inc(self.var_done, 1)

    def pool_rstd(self, eng, n):
        eng.wait_ge(self.var_done, self.upto(n))
        eng.tensor_tensor(self.c.rstd[:, :], self.c.var_eps[:, :], self.c.mhalf[:, :],
                          ALU.pow).then_inc(self.rstd_done, 1)

    def dve_scale(self, eng, n, par):
        c = self.c
        eng.wait_ge(self.rstd_done, self.upto(n))
        for t in range(T):
            ins = eng.tensor_scalar(c.h[:, par, t, :], c.x[:, n, t, :], c.moments[:, t, 0:1],
                                    c.rstd[:, t:t + 1], ALU.subtract, ALU.mult)
        ins.then_inc(self.scaled, 1)

    def dve_relu(self, eng, n, par):
        h = self.c.h[:, par, :, :]
        eng.wait_ge(self.scaled, self.upto(n))
        eng.tensor_scalar(h, h, 0.0, None, ALU.max).then_inc(self.h_ready, 1)

    def pe_turn(self, eng, n, par):
        c = self.c
        eng.wait_ge(self.h_ready, self.upto(n))
        for t in range(T):
            ins = eng.transpose(self.aux[:, t * P:(t + 1) * P], c.h[:, par, t, :], c.ident[:, :])
        ins.then_inc(self.h_turned, 1)

    def act_h_t(self, eng, n):
        eng.wait_ge(self.h_turned, self.upto(n))
        eng.activation(self.c.h_t[:, :], self.aux[:, :], ACT.Copy).then_inc(self.h_t_ready, 1)


def wait_apart(c, eng, sem, value):
    eng.wait_ge(sem, value)
    eng.sem_inc(c.passed, 1)


def walk(eng, prepare, stage, tail=lambda: None):
    prepare(0, 0)
    stage(0, 0, True, True)
    stage(1, 1, False, True)
    with eng.Fori(1, B // 2 - 1) as pair:
        stage(2 * pair, 0, False, True)
        stage(2 * pair + 1, 1, False, True)
    stage(B - 2, 0, False, True)
    stage(B - 1, 1, False, False)
    tail()


def project_nodes(eng, out, h_t, w):
    for t in range(T):
        ins = eng.matmul(out[:, t, :], h_t[:, t * P:(t + 1) * P], w, start=True, stop=True)
    return ins


def project_rows(eng, out, w, h_t):
    for i in range(2):
        ins = eng.matmul(out[:, i * HALF:(i + 1) * HALF], w, h_t[:, i * HALF:(i + 1) * HALF],
                         start=True, stop=True)
    return ins


def layer0(c, x_in, adj_t, w):
    nc = c.nc
    H, DH = 4, F // 4
    STEPS = 2 * T
    COPIES = 4
    STACK = 16 * COPIES * H
    SCALE = float(DH) ** -0.5
    with ExitStack() as ctx:
        sb = lambda name, shape, dt=F32: c.sb(name, shape, dt, ctx)
        bound = sb("bound", [P, T, N])
        chunk = sb("chunk", [P, T, HALF])
        pick = sb("pick", [P, T, 32])
        spread = sb("spread", [P, T, P])
        wq, wk, wv, wo = (sb(k, [P, F]) for k in ("wq", "wk", "wv", "wo"))
        bq, bk = sb("bq", [P, 1]), sb("bk", [P, 1])
        bv, bo, gamma, beta = (sb(k, [P, F]) for k in ("bv", "bo", "gamma", "beta"))
        split = sb("split", [P, 2, N], F32R)
        qs = [sb(f"qs{i}", [P, H, N], F32R) for i in range(2)]
        ks = [sb(f"ks{i}", [P, H, N], F32R) for i in range(2)]
        v = [sb(f"v{i}", [P, T, F]) for i in range(2)]
        e = sb("e", [P, 4, 2, HALF])
        adj_in = [chunk[:, :, :].rearrange("p (t a) n -> p t (a n)", t=4).bitcast(I32),
                  e[:, :, :, :].rearrange("p t a n -> p t (a n)").bitcast(I32)]
        inv_sum = sb("inv_sum", [P, HALF])
        ctx_sb = sb("ctx_sb", [P, 2, HALF])
        late = sb("late", [P, 4, F])
        u = c.h_t[:, 0:HALF].rearrange("p (t f) -> p t f", t=4)
        stats2, moments2 = sb("stats2", [P, 4, 6]), sb("moments2", [P, 4, 2])
        var2, rstd2 = sb("var2", [P, 4]), sb("rstd2", [P, 4])
        s_ps = c.ps("s_ps", [P, 2, 2, HALF], ctx)
        ctx_ps = c.ps("ctx_ps", [P, HALF], ctx)
        sum_ps = c.ps("sum_ps", [P, HALF], ctx)
        aux = c.ps("aux0", [P, N], ctx)
        aux_t = aux[:, :].rearrange("p (t f) -> p t f", t=T)

        loaded = c.sem("weights0_loaded")
        x_loaded = [c.sem(f"x_loaded_{k}") for k in ("0", "1", "2_on")]
        adj_loaded, bounded_above = [c.sem("adj_loaded_a"), c.sem("adj_loaded_b")], c.sem("bounded_above")
        bounded, consts, ident0 = c.sem("bounded"), c.sem("consts"), c.sem("ident_zeroed")
        nm = Norm(c, 0, aux)
        q_projected, q_hi, q_split, q_stacked = (c.sem(f"q_{k}") for k in ("projected", "hi", "split", "stacked"))
        k_projected, k_hi, k_split, k_stacked = (c.sem(f"k_{k}") for k in ("projected", "hi", "split", "stacked"))
        v_projected, v_ready, h_biased = c.sem("v_projected"), c.sem("v_ready"), c.sem("h_biased")
        s_ready, exp_done, p_ready, pv_done = (c.sem(k) for k in ("s_ready", "exp_done", "p_ready", "pv_done"))
        summed, inverted, chunk_copied, inv_spread, chunk_weighed, added, late_biased = (
            c.sem(k) for k in ("summed", "inverted", "chunk_copied", "inv_spread", "chunk_weighed", "added",
                               "late_biased"))
        o_projected, u_ready = c.sem("o_projected"), c.sem("u_ready")
        stats2_done, moments2_done, var2_done, rstd2_done, u_scaled, x_updated = (
            c.sem(k) for k in ("stats2_done", "moments2_done", "var2_done", "rstd2_done", "u_scaled", "x_updated0"))
        block = ctx.enter_context(nc.Block())

        def weighed_at(i):
            return int(1 <= i <= 8), (i - 1) % T

        @block.sync
        def _(sp):
            def load_x(b, done):
                sp.dma_start(c.x[:, b, :, :], x_in[b].rearrange("(t p) f -> p t f", p=P)).then_inc(done, 16)

            load_x(0, x_loaded[0])
            for dst, name in ((wq, "wq_t"), (wk, "wk_t"), (wv, "wv_t"), (wo, "wo_t"), (bq, "bq"), (bk, "bk")):
                sp.dma_start(dst[:, :], w[name]).then_inc(loaded, 16)
            for dst, name in ((bv, "bv"), (bo, "bo"), (gamma, "gamma"), (beta, "beta")):
                sp.dma_start(dst[:, :], w[name].partition_broadcast(P)).then_inc(loaded, 16)
            sp.dma_start(pick[:, :, :], w["pick"]).then_inc(loaded, 16)
            sp.dma_start(spread[:, :, :], w["spread"]).then_inc(loaded, 16)
            for t in range(T):
                sp.dma_start(adj_in[t // 4][:, t % 4, :], adj_t[t * P:(t + 1) * P, :]).then_inc(adj_loaded[t // 4], 16)
            for b in range(1, B):
                load_x(b, x_loaded[min(b, 2)])

            def stack(n, par, dst, parts, split_done, stacked):
                sp.wait_ge(split_done, n + 1)
                for copy in range(COPIES):
                    for h in range(H):
                        sp.dma_start(dst[par][copy * DH:(copy + 1) * DH, h, :].bitcast(F32),
                                     split[h * DH:(h + 1) * DH, parts[copy], :].bitcast(F32)).then_inc(stacked, 16)

            def prepare(n, par):
                wait_apart(c, sp, s_ready, 32 * n + 32)
                stack(n, par, qs, (0, 0, 1, 1), q_split, q_stacked)
                stack(n, par, ks, (0, 1, 0, 1), k_split, k_stacked)

            def stage(b, par, first, more):
                if more:
                    prepare(b + 1, 1 - par)

            walk(sp, prepare, stage)

        @block.gpsimd
        def _(pool):
            pool.memset(c.ident[:, :], 0.0).then_inc(ident0, 1)
            pool.memset(c.ones[:, :], 1.0)
            pool.memset(c.mhalf[:, :], -0.5)
            pool.wait_ge(ident0, 1)
            pool.affine_select(out=c.ident[:, :], in_=c.ident[:, :], compare_op=ALU.not_equal, fill=1.0, base=0,
                               pattern=[[-1, P]], channel_multiplier=1).then_inc(consts, 1)
            pool.wait_ge(consts, 1)
            pool.wait_ge(loaded, 192)

            def bias(n, par):
                pool.wait_ge(nm.h_turned, nm.upto(n))
                h0 = c.h[:, par, 0:4, :]
                pool.tensor_tensor(h0, h0, bo[:, :].unsqueeze(1).to_broadcast([P, 4, F]),
                                   ALU.add).then_inc(h_biased, 1)

            def bias_late(n, par):
                pool.wait_ge(u_ready, 2 * n + 2)
                pool.tensor_tensor(late[:, :, :], c.h[:, par, 4:8, :], bo[:, :].unsqueeze(1).to_broadcast([P, 4, F]),
                                   ALU.add).then_inc(late_biased, 1)

            def prepare(n, par):
                nm.pool_rstd(pool, n)
                bias(n, par)

            def rstd_out(b, half):
                pool.wait_ge(var2_done, 2 * b + half + 1)
                pool.tensor_tensor(rstd2[:, :], var2[:, :], c.mhalf[:, 0:4], ALU.pow).then_inc(rstd2_done, 1)

            def add(b, i):
                half, j = weighed_at(i)
                m = 2 * b + half - (0 if i >= 9 else 2)
                if j > 0:
                    pool.wait_ge(chunk_weighed, 8 * m + j + 9)
                    pool.wait_ge(added, 7 * m + j + 7)
                    acc = ctx_sb[:, half, :]
                    pool.tensor_tensor(acc, acc, chunk[:, j, :], ALU.add).then_inc(added, 1)

            def stage(b, par, first, more):
                for i in range(STEPS):
                    if not (first and i < 9):
                        add(b, i)
                    if more:
                        if i == 1:
                            nm.pool_rstd(pool, b + 1)
                        elif i == 8:
                            bias(b + 1, 1 - par)
                    if not first and i in (4, 15):
                        rstd_out(b - 1, i // 15)
                bias_late(b, par)

            def tail():
                for i in range(9):
                    add(B, i)
                    if i == 4:
                        rstd_out(B - 1, 0)
                rstd_out(B - 1, 1)

            pool.sem_inc(added, 8)
            walk(pool, prepare, stage, tail)

        @block.tensor
        def _(pe):
            pe.sem_inc(v_projected, 1)
            pe.sem_inc(s_ready, 64)
            pe.wait_ge(loaded, 192)
            pe.wait_ge(consts, 1)

            def turn(n, par):
                if not (isinstance(n, int) and n == 0):
                    pe.wait_ge(u_ready, 2 * n - 1)
                nm.pe_turn(pe, n, par)

            def q(n):
                pe.wait_ge(nm.h_t_ready, nm.upto(n))
                project_rows(pe, aux, wq[:, :], c.h_t).then_inc(q_projected, 1)

            def k(n):
                pe.wait_ge(q_split, n + 1)
                project_rows(pe, aux, wk[:, :], c.h_t).then_inc(k_projected, 1)

            def vv(n):
                pe.wait_ge(k_split, n + 1)
                project_nodes(pe, aux_t, c.h_t, wv[:, :]).then_inc(v_projected, 1)

            def prepare(n, par):
                turn(n, par)
                q(n)
                k(n)
                vv(n)

            def scores(b, par, i, hp):
                half, jt = divmod(i, T)
                pe.wait_ge(exp_done, 32 * b + 2 * i + hp + 1)
                for j in range(2):
                    ins = pe.matmul(s_ps[:, hp, j, :], ks[par][:, 2 * hp + j, jt * P:(jt + 1) * P],
                                    qs[par][:, 2 * hp + j, half * HALF:(half + 1) * HALF], start=True, stop=True)
                ins.then_inc(s_ready, 1)

            def sums(b, i):
                half, jt = divmod(i, T)
                pe.wait_ge(p_ready, 32 * b + 2 * i + 2)
                if jt == 0:
                    pe.wait_ge(inverted, 2 * b + half + 1)
                for h in range(H):
                    ins = pe.matmul(sum_ps[h * DH:(h + 1) * DH, :], pick[:, jt, :], e[:, 2 * (i % 2) + h // 2, h % 2, :],
                                    start=(jt == 0), stop=(jt == T - 1), tile_position=(0, h * DH))
                ins.then_inc(summed, 1)

            def spread_inverses(b, i):
                half, j = weighed_at(i)
                pe.wait_ge(inverted, 2 * b + half + (2 if i >= 9 else 0))
                pe.matmul(ctx_ps[:, :], spread[:, j, :], inv_sum[:, :], start=True, stop=True).then_inc(inv_spread, 1)

            def values(b, par, i):
                pe.wait_ge(chunk_copied, 16 * b + i + 1)
                pe.wait_ge(chunk_weighed, 16 * b + i + 1)
                for h in range(H):
                    ins = pe.matmul(ctx_ps[h * DH:(h + 1) * DH, :], v[par][:, i % T, h * DH:(h + 1) * DH],
                                    e[:, 2 * (i % 2) + h // 2, h % 2, :], start=True, stop=True,
                                    tile_position=(0, h * DH))
                ins.then_inc(pv_done, 1)

            def output(b, half):
                m = 2 * b + half
                pe.wait_ge(added, 7 * m + 15)
                pe.wait_ge(u_ready, m + 2)
                for t in range(4):
                    ins = pe.matmul(aux_t[:, t, :], ctx_sb[:, half, t * P:(t + 1) * P], wo[:, :], start=True, stop=True)
                ins.then_inc(o_projected, 1)

            def stacks(n):
                pe.wait_ge(q_stacked, STACK * (n + 1))
                pe.wait_ge(k_stacked, STACK * (n + 2))

            def stage(b, par, first, more):
                n = b + 1
                if first:
                    stacks(b)
                    for hp in range(2):
                        scores(b, par, 0, hp)
                    pe.wait_ge(v_ready, b + 1)
                for i in range(STEPS):
                    before = (b, par, i - 1) if i >= 1 else (b - 1, 1 - par, STEPS - 1)
                    after = (b, par, i + 1) if i + 1 < STEPS else (n, 1 - par, 0)
                    if not (first and i < 9):
                        pe.wait_ge(chunk_copied, 16 * b + i)
                        spread_inverses(b, i)
                    if not (first and i == 0):
                        sums(before[0], before[2])
                    if more or i + 1 < STEPS:
                        if i + 1 == STEPS:
                            stacks(n)
                        scores(*after, 0)
                    if not (first and i == 0):
                        values(*before)
                    if more or i + 1 < STEPS:
                        scores(*after, 1)
                    if not first and i == 2:
                        output(b - 1, 0)
                    if more:
                        if i == 5:
                            turn(n, 1 - par)
                        elif i == 7:
                            q(n)
                        elif i == 9:
                            k(n)
                        elif i == 11:
                            vv(n)
                    if i == 13:
                        if more:
                            pe.wait_ge(v_ready, n + 1)
                        if not first:
                            output(b - 1, 1)

            def tail():
                sums(B - 1, STEPS - 1)
                pe.wait_ge(chunk_copied, 16 * B)
                spread_inverses(B, 0)
                values(B - 1, 1, STEPS - 1)
                for i in range(1, 9):
                    if i == 1:
                        pe.wait_ge(chunk_copied, 16 * B + 1)
                    else:
                        pe.wait_ge(chunk_weighed, 16 * B + i - 1)
                    spread_inverses(B, i)
                    if i == 2:
                        output(B - 1, 0)
                output(B - 1, 1)

            walk(pe, prepare, stage, tail)

        @block.scalar
        def _(act):
            act.sem_inc(exp_done, 2)
            act.sem_inc(chunk_copied, 1)
            act.sem_inc(k_stacked, STACK)
            act.wait_ge(loaded, 192)

            def h_t(n):
                act.wait_ge(v_projected, n + 1)
                if not (isinstance(n, int) and n == 0):
                    act.wait_ge(x_updated, 2 * n - 1)
                nm.act_h_t(act, n)

            def high(n, projected, bias, done, free, value):
                act.wait_ge(projected, n + 1)
                act.wait_ge(free, value)
                act.activation(split[:, 0, :], aux[:, :], ACT.Identity, bias=bias[:, 0:1]).then_inc(done, 1)

            def q(n):
                high(n, q_projected, bq, q_hi, k_stacked, STACK * (n + 1))

            def k(n):
                high(n, k_projected, bk, k_hi, q_stacked, STACK * (n + 1))

            def prepare(n, par):
                h_t(n)
                q(n)
                k(n)
                act.wait_ge(bounded, 2)

            def exps(b, i, hp):
                act.wait_ge(s_ready, 32 * b + 2 * i + hp + 65)
                if hp == 0:
                    act.wait_ge(pv_done, 16 * b + i + 1)
                act.activation(e[:, 2 * (i % 2) + hp, :, :], s_ps[:, hp, :, :], ACT.Exp,
                               scale=SCALE).then_inc(exp_done, 1)

            def copy_chunk(b, i):
                act.wait_ge(pv_done, 16 * b + i + 3)
                act.wait_ge(added, 14 * b + 7 * (i // T) + i % T + 1)
                act.activation(chunk[:, i % T, :], ctx_ps[:, :], ACT.Copy).then_inc(chunk_copied, 1)

            def stage(b, par, first, more):
                n = b + 1
                for i in range(STEPS):
                    if i >= 2:
                        copy_chunk(b, i - 2)
                    elif not first:
                        copy_chunk(b - 1, i + STEPS - 2)
                    exps(b, i, 0)
                    exps(b, i, 1)
                    if more:
                        if i == 6:
                            h_t(n)
                        elif i == 8:
                            q(n)
                        elif i == 10:
                            k(n)

            def tail():
                copy_chunk(B - 1, STEPS - 2)
                copy_chunk(B - 1, STEPS - 1)

            act.sem_inc(pv_done, 2)
            walk(act, prepare, stage, tail)

        @block.vector
        def _(dve):
            dve.sem_inc(u_ready, 2)
            dve.sem_inc(x_updated, 2)
            dve.sem_inc(inverted, 1)
            dve.sem_inc(chunk_weighed, 8)
            dve.wait_ge(loaded, 192)
            dve.wait_ge(consts, 1)
            def bounds(part):
                dve.wait_ge(adj_loaded[part], 64)
                some = bound[:, 4 * part:4 * part + 4, :]
                dve.tensor_scalar(some, adj_in[part], 0, CLIP_HI, ALU.not_equal, ALU.mult).then_inc(bounded_above, 1)
                dve.wait_ge(bounded_above, part + 1)
                dve.tensor_scalar(some, some, CLIP_LO, None, ALU.max).then_inc(bounded, 1)

            def low(n, hi_done, bias, done):
                dve.wait_ge(hi_done, n + 1)
                dve.scalar_tensor_tensor(out=split[:, 1, :], in0=aux[:, :], scalar=bias[:, 0:1],
                                         in1=split[:, 0, :].bitcast(F32), op0=ALU.add,
                                         op1=ALU.subtract).then_inc(done, 1)

            def v_out(n, par):
                dve.wait_ge(v_projected, n + 2)
                for half in range(2):
                    sl = slice(4 * half, 4 * half + 4)
                    ins = dve.tensor_tensor(v[par][:, sl, :], aux_t[:, sl, :],
                                            bv[:, :].unsqueeze(1).to_broadcast([P, 4, F]), ALU.add)
                ins.then_inc(v_ready, 1)

            def prepare(n, par):
                dve.wait_ge(x_loaded[0], 16)
                nm.dve_stats(dve, n)
                nm.dve_moments(dve, n)
                nm.dve_scale(dve, n, par)
                nm.dve_relu(dve, n, par)
                low(n, q_hi, bq, q_split)
                low(n, k_hi, bk, k_split)
                v_out(n, par)
                bounds(0)
                bounds(1)
                dve.wait_ge(bounded, 2)

            def clip(b, i, hp):
                half, jt = divmod(i, T)
                dve.wait_ge(exp_done, 32 * b + 2 * i + hp + 3)
                tile = e[:, 2 * (i % 2) + hp, :, :]
                lim = bound[:, jt, half * HALF:(half + 1) * HALF].unsqueeze(1).to_broadcast([P, 2, HALF])
                dve.scalar_tensor_tensor(out=tile, in0=tile, scalar=CLIP_LO, in1=lim, op0=ALU.max,
                                         op1=ALU.min).then_inc(p_ready, 1)

            def invert(b, half):
                dve.wait_ge(summed, 16 * b + 8 * half + 8)
                dve.reciprocal(inv_sum[:, :], sum_ps[:, :]).then_inc(inverted, 1)

            def weigh(b, i):
                half, j = weighed_at(i)
                m = 2 * b + half - (0 if i >= 9 else 2)
                dve.wait_ge(inv_spread, 8 * m + j + 1)
                values = chunk[:, j, :]
                dve.tensor_tensor(ctx_sb[:, half, :] if j == 0 else values, values, ctx_ps[:, :],
                                  ALU.mult).then_inc(chunk_weighed, 1)

            def residual(b, par, half):
                m = 2 * b + half
                dve.wait_ge(o_projected, m + 1)
                dve.wait_ge(late_biased if half else h_biased, b + 1)
                dve.tensor_tensor(u[:, :, :], aux_t[:, 0:4, :], late[:, :, :] if half else c.h[:, par, 0:4, :],
                                  ALU.add).then_inc(u_ready, 1)
                dve.wait_ge(u_ready, m + 3)
                for t in range(4):
                    ins = dve.bn_stats(stats2[:, t, :], u[:, t, :])
                ins.then_inc(stats2_done, 1)
                wait_apart(c, dve, stats2_done, m + 1)
                for t in range(4):
                    ins = dve.bn_aggr(moments2[:, t, :], stats2[:, t, :])
                ins.then_inc(moments2_done, 1)
                dve.wait_ge(moments2_done, m + 1)
                dve.tensor_scalar(var2[:, :], moments2[:, :, 1], EPS, None, ALU.add).then_inc(var2_done, 1)

            def update(b, half):
                m = 2 * b + half
                dve.wait_ge(rstd2_done, m + 1)
                for t in range(4):
                    ins = dve.scalar_tensor_tensor(out=u[:, t, :], in0=u[:, t, :], scalar=moments2[:, t, 0:1],
                                                   in1=gamma[:, :], op0=ALU.subtract, op1=ALU.mult)
                    xt = c.x[:, b, 4 * half + t, :]
                    ins = dve.tensor_tensor(xt, xt, beta[:, :], ALU.add)
                ins.then_inc(u_scaled, 1)
                dve.wait_ge(u_scaled, m + 1)
                for t in range(4):
                    xt = c.x[:, b, 4 * half + t, :]
                    ins = dve.scalar_tensor_tensor(out=xt, in0=u[:, t, :], scalar=rstd2[:, t:t + 1], in1=xt,
                                                   op0=ALU.mult, op1=ALU.add)
                ins.then_inc(x_updated, 1)
                dve.wait_ge(x_updated, m + 3)

            def stage(b, par, first, more):
                n = b + 1
                if first:
                    dve.wait_ge(x_loaded[1], 16)
                elif isinstance(b, int) and b == 1:
                    dve.wait_ge(x_loaded[2], 16 * (B - 2))
                for i in range(STEPS):
                    if not (first and i < 9):
                        weigh(b, i)
                    clip(b, i, 0)
                    if i == 8:
                        invert(b, 0)
                    elif i == 0 and not first:
                        invert(b - 1, 1)
                    clip(b, i, 1)
                    if not first:
                        if i == 3:
                            residual(b - 1, 1 - par, 0)
                        elif i == 5:
                            update(b - 1, 0)
                        elif i == 14:
                            residual(b - 1, 1 - par, 1)
                        elif i == 15:
                            update(b - 1, 1)
                    if more:
                        if i == 0:
                            nm.dve_stats(dve, n)
                        elif i == 1:
                            nm.dve_moments(dve, n)
                        elif i == 4:
                            if not first:
                                dve.wait_ge(late_biased, b)
                            nm.dve_scale(dve, n, 1 - par)
                            nm.dve_relu(dve, n, 1 - par)
                        elif i == 8:
                            low(n, q_hi, bq, q_split)
                        elif i == 10:
                            low(n, k_hi, bk, k_split)
                        elif i == 12:
                            v_out(n, 1 - par)

            def tail():
                for i in range(9):
                    weigh(B, i)
                    if i == 0:
                        invert(B - 1, 1)
                    elif i == 4:
                        residual(B - 1, 1, 0)
                        update(B - 1, 0)
                residual(B - 1, 1, 1)
                update(B - 1, 1)

            walk(dve, prepare, stage, tail)


def additive_layer(c, layer, H, w):
    nc = c.nc
    DH = F // H
    W1 = DH + 1
    NC = 2 * W1
    NS = 3 * NC
    OWN = 2
    SC = T - OWN
    RING = 4
    L = str(layer)
    with ExitStack() as ctx:
        sb = lambda name, shape, dt=F32: c.sb(name + L, shape, dt, ctx)
        wv = sb("wv", [P, F])
        a_row = sb("a_row", [P, 2, F])
        wa_prod, wa = sb("wa_prod", [P, 2, F]), sb("wa", [P, 2, H])
        prior = sb("prior", [P, 1])
        wh = sb("wh", [P, T, H, DH])
        sd = sb("sd", [P, T, 2, H])
        s_row = sb("s_row", [H, N])
        top_part, top = sb("top_part", [P, H]), sb("top", [P, H])
        z, dz = sb("z", [P, T, H]), sb("dz", [P, T, H])
        z_up, z_down = sb("z_up", [P, T, H]), sb("z_down", [P, T, H])
        up = [sb(f"up{i}_", [P, T, H]) for i in range(2)]
        down = [sb(f"down{i}_", [P, T, H]) for i in range(2)]
        keyf = sb("keyf", [P, T, H, 2])
        steep_d = [sb(f"steep_d{i}_", [P, T, H]) for i in range(2)]
        minus_d = [sb(f"minus_d{i}_", [P, T, H]) for i in range(2)]
        vals = sb("vals", [P, T, H, 2, W1])
        parts = [sb(f"parts{i}_", [P, T, H, 3, 2, W1], BF16) for i in range(2)]
        s_all = sb("s_all", [P, 2, N])
        steep = sb("steep", [P, 4, N], BF16)
        g = [sb(f"g{i}_", [P, T, N], BF16) for i in range(2)]
        sums = [sb(f"sums{i}_", [P, H, T, 2, W1]) for i in range(2)]
        base = [sb(f"base{i}_", [P, T, H, W1]) for i in range(2)]
        pr = sb("pr", [P, 8])
        inv = sb("inv", [P, H, T])
        out = sb("out", [P, T, F])
        neg = sb("neg", [P, T, F])
        acc = c.ps("acc" + L, [P, 4, HALF], ctx)
        post = c.ps("post" + L, [P, 2, HALF], ctx)
        aux = c.ps("aux" + L, [P, N], ctx)
        aux_t = aux[:, :].rearrange("p (t f) -> p t f", t=T)
        s_dram = c.nc.dram_tensor("s_rows" + L, (2, H, N), F32, kind="Internal").ap()
        if layer == 2:
            w_out = sb("w_out", [P, F])
            out_t = sb("out_t", [P, N])
            post_t = post[:, :, :].rearrange("p a (t f) -> p (a t) f", f=F)

        sem = lambda name: c.sem(name + L)
        nm = Norm(c, layer, aux)
        if layer == 1:
            adj_in = [m[:, :, :].rearrange("p t n -> p (t n)").bitcast(I32).rearrange("p (t n) -> p t n", t=4)
                      for m in g]
            adj_loaded, edge_ready = sem("adj_loaded"), sem("edge_ready")
        loaded, wa_mult, wa_ready = (sem(k) for k in ("loaded", "wa_mult", "wa_ready"))
        v_projected, wh_ready, sd_projected, sd_ready, row_projected, row_ready = (
            sem(k) for k in ("v_projected", "wh_ready", "sd_projected", "sd_ready", "row_projected", "row_ready"))
        row_stored, s_loaded = sem("row_stored"), [sem("s_loaded_a"), sem("s_loaded_b")]
        top_partial, top_ready, z_ready, z_parts, factors = (
            sem(k) for k in ("top_partial", "top_ready", "z_ready", "z_parts", "factors"))
        vals_ready, hi_ready, rest1, mid_ready, parts_ready = (
            sem(k) for k in ("vals_ready", "hi_ready", "rest1", "mid_ready", "parts_ready"))
        base_summed, base_ready = sem("base_summed"), sem("base_ready")
        steep_ready, g_ready, acc_summed, acc_read = (
            sem(k) for k in ("steep_ready", "g_ready", "acc_summed", "acc_read"))
        scaled_sums, downs, totals, inverted, out_ready = (
            sem(k) for k in ("scaled_sums", "downs", "totals", "inverted", "out_ready"))
        x_updated = sem("x_updated")
        if layer == 1:
            neg_ready, exp_ready, x_relu = (sem(k) for k in ("neg_ready", "exp_ready", "x_relu"))
        else:
            prior_steps, prior_ready, out_turned, out_t_ready, out_projected = (
                sem(k) for k in ("prior_steps", "prior_ready", "out_turned", "out_t_ready", "out_projected"))
        block = ctx.enter_context(nc.Block())

        def part(par, k):
            return parts[par][:, :, :, k, :, :].rearrange("p t h k c -> p (t h) (k c)")

        def all_vals():
            return vals[:, :, :, :, :].rearrange("p t h k c -> p (t h) (k c)")

        def pieces(table, slot, n, par):
            for step in table.get(slot, ()):
                step(n, par)

        @block.sync
        def _(sp):
            sp.dma_start(wv[:, :], w["wv"]).then_inc(loaded, 16)
            for k in range(2):
                sp.dma_start(a_row[:, k, :], w["a"][k].partition_broadcast(P)).then_inc(loaded, 16)
            if layer == 2:
                sp.dma_start(w_out[:, :], w["w_out_t"]).then_inc(loaded, 16)
                sp.dma_start(pr[:, 0:1], w["beta_tilde"].partition_broadcast(P)).then_inc(loaded, 16)
            if layer == 1:
                for t in range(T):
                    sp.dma_start(adj_in[t // 4][:, t % 4, :], w["adj_t"][t * P:(t + 1) * P, :]).then_inc(adj_loaded, 16)
            sp.sem_inc(row_stored, 16)

            def prepare(n, par):
                sp.wait_ge(row_ready, n + 2)
                sp.dma_start(s_dram[par], s_row[:, :]).then_inc(row_stored, 16)

            def stage(b, par, first, more):
                sp.wait_ge(row_stored, 16 * b + 32)
                for h in range(H):
                    if more and H == 8 and h == H - 1:
                        prepare(b + 1, 1 - par)
                    sp.wait_ge(g_ready, T * (H * b + h) + T)
                    sp.dma_start(s_all[:, h % 2, :], s_dram[par, h, :].partition_broadcast(P)).then_inc(s_loaded[h % 2], 16)
                if more and H == 4:
                    prepare(b + 1, 1 - par)

            walk(sp, prepare, stage, lambda: None)

        @block.gpsimd
        def _(pool):
            def prepare_parts(n, par):
                wait_apart(c, pool, top_partial, n + 1)
                pool.partition_all_reduce(top[:, :], top_part[:, :], P, RMAX).then_inc(top_ready, 1)
                pool.wait_ge(hi_ready, n + 1)
                pool.tensor_tensor(all_vals(), all_vals(), part(par, 0), ALU.subtract).then_inc(rest1, 1)
                pool.wait_ge(mid_ready, n + 1)
                pool.tensor_tensor(part(par, 2), all_vals(), part(par, 1), ALU.subtract).then_inc(parts_ready, 1)

            def prepare(n, par):
                nm.pool_rstd(pool, n)
                prepare_parts(n, par)

            def combine(b, par):
                pool.wait_ge(acc_read, 4 * H * (b + 1) + 4)
                pool.wait_ge(base_ready, T * (b + 1))
                sm = sums[par]
                for h in range(H):
                    pool.tensor_tensor(sm[:, h, :, 0, :], sm[:, h, :, 0, :],
                                       up[par][:, :, h].unsqueeze(2).to_broadcast([P, T, W1]), ALU.mult)
                    ins = pool.tensor_tensor(sm[:, h, :, 1, :], base[par][:, :, h, :], sm[:, h, :, 1, :], ALU.subtract)
                ins.then_inc(scaled_sums, 1)
                pool.wait_ge(scaled_sums, b + 1)
                for h in range(H):
                    ins = pool.tensor_tensor(sm[:, h, :, 1, :], sm[:, h, :, 1, :],
                                             down[par][:, :, h].unsqueeze(2).to_broadcast([P, T, W1]), ALU.mult)
                ins.then_inc(downs, 1)
                pool.wait_ge(downs, b + 1)
                both = sm[:, :, :, :, :].rearrange("p h t k c -> p (h t) k c")
                pool.tensor_tensor(both[:, :, 0, :], both[:, :, 0, :], both[:, :, 1, :], ALU.add).then_inc(totals, 1)

            def stage(b, par, first, more):
                if more:
                    nm.pool_rstd(pool, b + 1)
                if not first:
                    combine(b - 1, 1 - par)
                if more:
                    prepare_parts(b + 1, 1 - par)

            walk(pool, prepare, stage, lambda: combine(B - 1, 1))

        @block.tensor
        def _(pe):
            pe.sem_inc(acc_summed, 8)
            pe.wait_ge(loaded, 16 * (5 if layer == 2 else 3))
            pe.wait_ge(wa_ready, 1)

            def turn(n, par):
                pe.wait_ge(row_ready, n + 1)
                nm.pe_turn(pe, n, par)

            def values(n, par):
                pe.wait_ge(nm.h_t_ready, nm.upto(n))
                project_nodes(pe, aux_t, c.h_t, wv[:, :]).then_inc(v_projected, 1)

            def columns(n, par):
                pe.wait_ge(wh_ready, n + 1)
                for t in range(T):
                    ins = pe.matmul(aux[:, t * 2 * H:(t + 1) * 2 * H], c.h_t[:, t * P:(t + 1) * P],
                                    wa[:, :, :].rearrange("p k h -> p (k h)"), start=True, stop=True)
                ins.then_inc(sd_projected, 1)

            def rows(n, par):
                pe.wait_ge(sd_ready, n + 1)
                for i in range(2):
                    ins = pe.matmul(aux[0:H, i * HALF:(i + 1) * HALF], wa[:, 0, :],
                                    c.h_t[:, i * HALF:(i + 1) * HALF], start=True, stop=True)
                ins.then_inc(row_projected, 1)

            def prepare(n, par):
                for step in (turn, values, columns, rows):
                    step(n, par)

            table = {2: [turn], 3: [values], 4: [columns], 5: [rows]}

            def bases(b, par):
                for it in range(T):
                    if it >= 2:
                        pe.wait_ge(base_ready, T * b + it - 1)
                    for jt in range(T):
                        ins = pe.matmul(post[:, it % 2, 0:H * 3 * W1].rearrange("p (h k c) -> p h k c", h=H, k=3),
                                        c.edge[:, jt, it * P:(it + 1) * P], parts[par][:, jt, :, :, 1, :],
                                        start=(jt == 0), stop=(jt == T - 1))
                    ins.then_inc(base_summed, 1)

            def head(b, par, h, its):
                if its[0] == 0:
                    pe.wait_ge(g_ready, T * (H * b + h) + 3 * T)
                for it in its:
                    if it % 2 == 0:
                        pe.wait_ge(acc_read, 4 * (H * b + h) + it // 2 + 1)
                    o = (it % 2) * NS
                    for jt in range(T):
                        ins = pe.matmul(acc[:, it // 2, o:o + NS], g[h % 2][:, jt, it * P:(it + 1) * P],
                                        parts[par][:, jt, h, :, :, :].rearrange("p k a c -> p (k a c)"),
                                        start=(jt == 0), stop=(jt == T - 1))
                    if it % 2 == 1:
                        ins.then_inc(acc_summed, 1)

            def out_turn(b):
                pe.wait_ge(out_ready, b + 1)
                for t in range(T):
                    ins = pe.transpose(post_t[:, t, :], out[:, t, :], c.ident[:, :])
                ins.then_inc(out_turned, 1)

            def out_project(b):
                pe.wait_ge(out_t_ready, b + 1)
                project_nodes(pe, post_t, out_t, w_out[:, :]).then_inc(out_projected, 1)

            def stage(b, par, first, more):
                for h in range(H):
                    if h == 0:
                        pe.wait_ge(parts_ready, b + 1)
                    head(b, par, h, range(T // 2))
                    if more and H == 4:
                        pieces(table, 2 * h + 1, b + 1, 1 - par)
                    head(b, par, h, range(T // 2, T))
                    if more:
                        pieces(table, 2 * h + 2 if H == 4 else h + 1, b + 1, 1 - par)
                    if h == 0:
                        bases(b, par)
                    if layer == 2 and not first:
                        if h == 3:
                            pe.wait_ge(base_ready, T * b + T)
                            out_turn(b - 1)
                        elif h == 4:
                            out_project(b - 1)

            def tail():
                if layer == 2:
                    out_turn(B - 1)
                    out_project(B - 1)

            walk(pe, prepare, stage, tail)

        @block.scalar
        def _(act):
            act.sem_inc(row_ready, 1)
            if layer == 2:
                act.wait_ge(prior_steps, 2)
                act.activation(pr[:, 3:4], pr[:, 2:3], ACT.Exp, scale=-1.0).then_inc(prior_ready, 1)
                act.wait_ge(prior_ready, 1)
                act.activation(pr[:, 4:5], pr[:, 3:4], ACT.Ln, bias=c.ones[:, 0:1])
                act.activation(pr[:, 6:7], c.ones[:, 0:1], ACT.Ln, bias=pr[:, 5:6]).then_inc(prior_ready, 1)
            act.wait_ge(wa_ready, 1)

            def copy(out_ap, in_ap, done):
                act.activation(out_ap, in_ap, ACT.Copy).then_inc(done, 1)

            def h_t(n, par):
                nm.act_h_t(act, n)

            def wh_out(n, par):
                act.wait_ge(v_projected, n + 1)
                copy(wh[:, :, :, :].rearrange("p t h d -> p (t h d)"), aux[:, :], wh_ready)

            def row_out(n, par):
                act.wait_ge(row_projected, n + 1)
                act.wait_ge(row_stored, 16 * n + 16)
                copy(s_row[:, :], aux[0:H, :], row_ready)

            def exps(n, par):
                act.wait_ge(z_parts, n + 1)
                act.activation(up[par][:, :, :], z_up[:, :, :], ACT.Exp)
                act.activation(down[par][:, :, :], z_down[:, :, :], ACT.Exp)
                act.activation(keyf[:, :, :, 0], dz[:, :, :], ACT.Exp, bias=prior[:, 0:1])
                act.activation(keyf[:, :, :, 1], dz[:, :, :], ACT.Exp, bias=prior[:, 0:1],
                               scale=0.2).then_inc(factors, 1)

            def hi(n, par):
                act.wait_ge(vals_ready, n + 1)
                copy(part(par, 0), all_vals(), hi_ready)

            def mid(n, par):
                act.wait_ge(rest1, n + 1)
                copy(part(par, 1), all_vals(), mid_ready)

            def prepare(n, par):
                for step in (h_t, wh_out, row_out, exps, hi, mid):
                    step(n, par)

            if H == 4:
                table = {2: [h_t], 4: [wh_out], 6: [row_out, exps], 7: [hi, mid]}
            else:
                table = {2: [h_t], 3: [wh_out], 5: [row_out, exps], 6: [hi], 7: [mid]}

            def compare(b, par, h, jt):
                x = T * (H * b + h) + 2 * T
                act.wait_ge(g_ready, x + OWN + jt - RING + 1 if jt >= RING else x - T + OWN + SC + jt - RING + 1)
                act.activation(steep[:, (SC * h + jt) % RING, :], s_all[:, h % 2, :], ACT.Relu,
                               bias=steep_d[par][:, jt, h:h + 1], scale=STEEP).then_inc(steep_ready, 1)

            def neg_exp(b):
                act.wait_ge(neg_ready, b + 1)
                act.activation(neg[:, :, :], neg[:, :, :], ACT.Exp).then_inc(exp_ready, 1)

            def out_t_copy(b):
                act.wait_ge(out_turned, b + 1)
                copy(out_t[:, :], post[:, :, :].rearrange("p a n -> p (a n)"), out_t_ready)

            def stage(b, par, first, more):
                for h in range(H):
                    act.wait_ge(s_loaded[h % 2], 16 * (H // 2) * b + 16 * (h // 2) + 16)
                    for jt in range(SC):
                        compare(b, par, h, jt)
                        if more and H == 4 and jt == SC // 2 - 1:
                            pieces(table, 2 * h, b + 1, 1 - par)
                    if more:
                        pieces(table, 2 * h + 1 if H == 4 else h, b + 1, 1 - par)
                    if not first:
                        if layer == 1 and h == 3:
                            neg_exp(b - 1)
                        elif layer == 2 and h == 4:
                            out_t_copy(b - 1)

            walk(act, prepare, stage, lambda: neg_exp(B - 1) if layer == 1 else out_t_copy(B - 1))

        @block.vector
        def _(dve):
            dve.sem_inc(g_ready, 2 * T)
            dve.sem_inc(acc_read, 4)
            dve.wait_ge(loaded, 16 * (5 if layer == 2 else 3))
            if layer == 2:
                dve.tensor_scalar(pr[:, 1:2], pr[:, 0:1], -1.0, None, ALU.mult).then_inc(prior_steps, 1)
                dve.wait_ge(prior_steps, 1)
                dve.memset(pr[:, 5:6], 1e-6)
                dve.tensor_tensor(pr[:, 2:3], pr[:, 0:1], pr[:, 1:2], ALU.max).then_inc(prior_steps, 1)
                dve.wait_ge(prior_ready, 2)
                dve.scalar_tensor_tensor(out=pr[:, 7:8], in0=pr[:, 0:1], scalar=0.0, in1=pr[:, 4:5], op0=ALU.max,
                                         op1=ALU.add).then_inc(prior_steps, 1)
                dve.wait_ge(prior_steps, 3)
                dve.tensor_tensor(prior[:, :], pr[:, 7:8], pr[:, 6:7], ALU.mult)
            else:
                dve.memset(prior[:, :], 0.0)
            for k in range(2):
                ins = dve.tensor_tensor(wa_prod[:, k, :], wv[:, :], a_row[:, k, :], ALU.mult)
            ins.then_inc(wa_mult, 1)
            dve.wait_ge(wa_mult, 1)
            dve.tensor_reduce(wa[:, :, :], wa_prod[:, :, :].rearrange("p k (h d) -> p k h d", h=H), AX.X,
                              ALU.add).then_inc(wa_ready, 1)

            def stats(n, par):
                nm.dve_stats(dve, n)
                nm.dve_moments(dve, n)

            def scale(n, par):
                nm.dve_scale(dve, n, par)
                nm.dve_relu(dve, n, par)

            def sd_out(n, par):
                dve.wait_ge(sd_projected, n + 1)
                dve.tensor_copy(sd[:, :, :, :].rearrange("p t k h -> p (t k h)"), aux[:, 0:T * 2 * H]).then_inc(sd_ready, 1)
                dve.wait_ge(sd_ready, n + 1)
                dve.tensor_reduce(top_part[:, :], sd[:, :, 1, :].rearrange("p t h -> p h t"), AX.X,
                                  ALU.max).then_inc(top_partial, 1)

            def zs(n, par):
                dve.wait_ge(top_ready, n + 1)
                all_top = top[:, :].unsqueeze(1).to_broadcast([P, T, H])
                dve.tensor_tensor(z[:, :, :], sd[:, :, 0, :], all_top, ALU.add)
                dve.tensor_tensor(dz[:, :, :], sd[:, :, 1, :], all_top, ALU.subtract).then_inc(z_ready, 1)
                dve.wait_ge(z_ready, n + 1)
                dve.tensor_scalar(z_up[:, :, :], z[:, :, :], 0.8, 0.0, ALU.mult, ALU.min)
                dve.tensor_scalar(z_down[:, :, :], z[:, :, :], -0.8, 0.0, ALU.mult, ALU.min)
                dve.tensor_scalar(steep_d[par][:, :, :], sd[:, :, 1, :], STEEP, None, ALU.mult)
                dve.tensor_scalar(minus_d[par][:, :, :], sd[:, :, 1, :], -1.0, None, ALU.mult).then_inc(z_parts, 1)

            def weigh(n, par):
                dve.wait_ge(factors, n + 1)
                dve.wait_ge(wh_ready, n + 1)
                to = vals[:, :, :, :, :].rearrange("p t h k c -> p (t h) k c")
                f = keyf[:, :, :, :].rearrange("p t h k -> p (t h) k")
                for k in range(2):
                    dve.tensor_tensor(to[:, :, k, 0:DH], wh[:, :, :, :].rearrange("p t h d -> p (t h) d"),
                                      f[:, :, k:k + 1].to_broadcast([P, T * H, DH]), ALU.mult)
                dve.tensor_copy(to[:, :, :, DH], f).then_inc(vals_ready, 1)

            def prepare(n, par):
                for step in (stats, scale, sd_out, zs, weigh):
                    step(n, par)
                if layer == 1:
                    dve.wait_ge(adj_loaded, 16 * T)
                    for i in range(2):
                        ins = dve.tensor_scalar(c.edge[:, 4 * i:4 * i + 4, :], adj_in[i], 0, None, ALU.is_gt)
                    ins.then_inc(edge_ready, 1)
                    dve.wait_ge(edge_ready, 1)

            if H == 4:
                table = {0: [stats], 1: [scale], 5: [sd_out], 6: [zs], 7: [weigh]}
            else:
                table = {0: [stats], 1: [scale], 4: [sd_out], 5: [zs], 6: [weigh]}

            def read_sums(b, par, h, pair):
                dve.wait_ge(acc_summed, 4 * (H * b + h) + pair + 9)
                dve.tensor_reduce(sums[par][:, h, 2 * pair:2 * pair + 2, :, :].rearrange("p i k c -> p i (k c)"),
                                  acc[:, pair, 0:2 * NS].rearrange("p (i k c) -> p i c k", i=2, k=3),
                                  AX.X, ALU.add).then_inc(acc_read, 1)

            def read_base(b, par, it):
                dve.wait_ge(base_summed, T * b + it + 1)
                dve.tensor_reduce(base[par][:, it, :, :],
                                  post[:, it % 2, 0:H * 3 * W1].rearrange("p (h k c) -> p h c k", h=H, k=3),
                                  AX.X, ALU.add).then_inc(base_ready, 1)

            def post_a(b, par):
                dve.wait_ge(totals, b + 1)
                dve.reciprocal(inv[:, :, :], sums[par][:, :, :, 0, DH]).then_inc(inverted, 1)
                dve.wait_ge(inverted, b + 1)
                dve.tensor_tensor(out[:, :, :].rearrange("p t (h d) -> p h t d", h=H), sums[par][:, :, :, 0, 0:DH],
                                  inv[:, :, :].unsqueeze(3).to_broadcast([P, H, T, DH]), ALU.mult).then_inc(out_ready, 1)
                if layer == 1:
                    dve.wait_ge(out_ready, b + 1)
                    dve.tensor_scalar(neg[:, :, :], out[:, :, :], 0.0, None, ALU.min).then_inc(neg_ready, 1)

            def post_b(b):
                xb = c.x[:, b, :, :]
                if layer == 1:
                    dve.scalar_tensor_tensor(out=xb, in0=out[:, :, :], scalar=0.0, in1=xb, op0=ALU.max,
                                             op1=ALU.add).then_inc(x_relu, 1)
                    dve.wait_ge(x_relu, b + 1)
                    dve.wait_ge(exp_ready, b + 1)
                    dve.scalar_tensor_tensor(out=xb, in0=neg[:, :, :], scalar=-1.0, in1=xb, op0=ALU.add,
                                             op1=ALU.add).then_inc(x_updated, 1)
                else:
                    dve.wait_ge(out_projected, b + 1)
                    dve.tensor_tensor(xb, xb, post_t, ALU.add).then_inc(x_updated, 1)
                dve.wait_ge(x_updated, b + 1)

            def make_g(b, par, h, step):
                x = H * b + h
                if step < OWN:
                    jt = SC + step
                    if step == 0:
                        dve.wait_ge(s_loaded[h % 2], 16 * (H // 2) * b + 16 * (h // 2) + 16)
                        dve.wait_ge(acc_summed, 4 * x + 4)
                    dve.scalar_tensor_tensor(out=g[h % 2][:, jt, :], in0=s_all[:, h % 2, :],
                                             scalar=minus_d[par][:, jt, h:h + 1], in1=c.edge[:, jt, :],
                                             op0=ALU.is_gt, op1=ALU.mult).then_inc(g_ready, 1)
                else:
                    jt = step - OWN
                    dve.wait_ge(steep_ready, SC * x + jt + 1)
                    dve.tensor_tensor(g[h % 2][:, jt, :], steep[:, (SC * h + jt) % RING, :], c.edge[:, jt, :],
                                      ALU.min).then_inc(g_ready, 1)

            def stage(b, par, first, more):
                for h in range(H):
                    for step in range(T):
                        make_g(b, par, h, step)
                        if step in (2, 4, 6, 7):
                            pair = (2, 4, 6, 7).index(step)
                            if h > 0:
                                read_sums(b, par, h - 1, pair)
                            elif not first:
                                read_sums(b - 1, 1 - par, H - 1, pair)
                        if h == 1:
                            read_base(b, par, step)
                        if more and H == 4 and step == 3:
                            pieces(table, 2 * h, b + 1, 1 - par)
                    if more:
                        pieces(table, 2 * h + 1 if H == 4 else h, b + 1, 1 - par)
                    if not first:
                        if h == 2:
                            post_a(b - 1, 1 - par)
                        elif h == (3 if H == 4 else 6):
                            post_b(b - 1)

            def tail():
                for pair in range(4):
                    read_sums(B - 1, 1, H - 1, pair)
                post_a(B - 1, 1)
                post_b(B - 1)

            walk(dve, prepare, stage, tail)


def layer3(c, x_out, adj, w):
    nc = c.nc
    KEEP = 4
    with ExitStack() as ctx:
        sb = lambda name, shape, dt=F32: c.sb(name, shape, dt, ctx)
        adj_in = sb("adj_in3", [P, 2, N], I32)
        bias = sb("bias3", [P, T, N], BF16)
        w1, w2, w3 = (sb(k, [P, F]) for k in ("w1", "w2", "w3"))
        q = [sb(f"q3_{i}", [P, N]) for i in range(2)]
        k = [sb(f"k3_{i}", [P, N]) for i in range(2)]
        v = [sb(f"v3_{i}", [P, T, F]) for i in range(2)]
        z = sb("z3", [P, 2, N])
        zt = sb("zt3", [P, T, P])
        top, minus, shift = sb("top3", [P, 2]), sb("minus3", [P, 2]), sb("shift3", [P, 2])
        total, inv = sb("total3", [P, KEEP]), sb("inv3", [P, KEEP])
        res = sb("res3", [P, F])
        s_ps = c.ps("s3_ps", [P, N], ctx)
        t_ps = c.ps("t3_ps", [P, 2, HALF], ctx)
        o_ps = c.ps("o3_ps", [P, 2, HALF], ctx)
        aux = c.ps("aux3", [P, N], ctx)
        aux_t = aux[:, :].rearrange("p (t f) -> p t f", t=T)

        sem = lambda name: c.sem(name + "3")
        nm = Norm(c, 3, aux)
        loaded, adj_loaded, adj_used = sem("weights"), [sem("adj_a"), sem("adj_b")], sem("adj_used")
        q_projected, q_ready, k_projected, k_ready, v_projected, v_ready = (
            sem(s) for s in ("q_projected", "q_ready", "k_projected", "k_ready", "v_projected", "v_ready"))
        s_ready, biased, minus_ready, shift_ready, leaky = (
            sem(s) for s in ("s_ready", "biased", "minus_ready", "shift_ready", "leaky"))
        exp_done, turned, zt_low, zt_high, o_ready = (
            sem(s) for s in ("exp_done", "turned", "zt_low", "zt_high", "o_ready"))
        inverted, res_ready, x_updated, stored = (sem(s) for s in ("inverted", "res_ready", "x_updated", "stored"))
        block = ctx.enter_context(nc.Block())

        @block.sync
        def _(sp):
            for dst, name in ((w1, "w1"), (w2, "w2"), (w3, "w3")):
                sp.dma_start(dst[:, :], w[name]).then_inc(loaded, 16)
            for t in range(T):
                if t >= 2:
                    sp.wait_ge(adj_used, t - 1)
                sp.dma_start(adj_in[:, t % 2, :], adj[t * P:(t + 1) * P, :]).then_inc(adj_loaded[t % 2], 16)

            def store(b):
                wait_apart(c, sp, x_updated, T * (b + 1))
                sp.dma_start(x_out[b].rearrange("(t p) f -> p t f", p=P), c.x[:, b, :, :]).then_inc(stored, 16)

            def stage(b, par, first, more):
                if not first:
                    store(b - 1)

            walk(sp, lambda n, par: None, stage, lambda: store(B - 1))
            sp.wait_ge(stored, 16 * B)

        @block.gpsimd
        def _(pool):
            def stage(b, par, first, more):
                if more:
                    nm.pool_rstd(pool, b + 1)

            walk(pool, lambda n, par: nm.pool_rstd(pool, n), stage)

        @block.tensor
        def _(pe):
            pe.wait_ge(loaded, 48)

            def turn(n, par):
                if not (isinstance(n, int) and n == 0):
                    pe.wait_ge(v_ready, n)
                nm.pe_turn(pe, n, par)

            def q_rows(n, par):
                pe.wait_ge(nm.h_t_ready, nm.upto(n))
                project_rows(pe, aux, w1[:, :], c.h_t).then_inc(q_projected, 1)

            def k_rows(n, par):
                pe.wait_ge(q_ready, n + 1)
                project_rows(pe, aux, w2[:, :], c.h_t).then_inc(k_projected, 1)

            def v_nodes(n, par):
                pe.wait_ge(k_ready, n + 1)
                project_nodes(pe, aux_t, c.h_t, w3[:, :]).then_inc(v_projected, 1)

            def prepare(n, par):
                for step in (turn, q_rows, k_rows, v_nodes):
                    step(n, par)

            table = {1: turn, 2: q_rows, 3: k_rows, 5: v_nodes}

            def scores(m, par, i):
                if not (isinstance(m, int) and m == 0):
                    pe.wait_ge(biased, m)
                for j in range(2):
                    ins = pe.matmul(s_ps[:, j * HALF:(j + 1) * HALF], q[par][:, i * P:(i + 1) * P],
                                    k[par][:, j * HALF:(j + 1) * HALF], start=True, stop=True)
                ins.then_inc(s_ready, 1)

            def turn_weights(m, i):
                pe.wait_ge(exp_done, m + 1)
                if not (isinstance(m, int) and m == 0):
                    pe.wait_ge(zt_low, m)
                    pe.wait_ge(zt_high, m)
                for t in range(T):
                    ins = pe.transpose(t_ps[:, t // 4, (t % 4) * P:(t % 4 + 1) * P], z[:, i % 2, t * P:(t + 1) * P],
                                       c.ident[:, :])
                ins.then_inc(turned, 1)

            def values(m, par, i):
                pe.wait_ge(zt_low, m + 1)
                pe.wait_ge(zt_high, m + 1)
                for t in range(T):
                    ins = pe.matmul(o_ps[:, i % 2, 0:F], zt[:, t, :], v[par][:, t, :], start=(t == 0), stop=(t == T - 1))
                ins.then_inc(o_ready, 1)

            def step(b, par, i, first):
                m = T * b + i
                if i < T:
                    scores(m, par, i)
                if not (first and i < 2):
                    values(m - 2, par if i >= 2 else 1 - par, i % 2)
                if not (first and i < 1) and i < T + 1:
                    turn_weights(m - 1, (i + 1) % 2)

            def stage(b, par, first, more):
                pe.wait_ge(q_ready, b + 1)
                pe.wait_ge(k_ready, b + 1)
                pe.wait_ge(v_ready, b + 1)
                for i in range(T):
                    step(b, par, i, first)
                    if more and i in table:
                        table[i](b + 1, 1 - par)

            def tail():
                step(B - 1, 1, T, False)
                step(B - 1, 1, T + 1, False)

            walk(pe, prepare, stage, tail)

        @block.scalar
        def _(act):
            def h_t(n, par):
                nm.act_h_t(act, n)

            def q_out(n, par):
                act.wait_ge(q_projected, n + 1)
                act.activation(q[par][:, :], aux[:, :], ACT.Copy).then_inc(q_ready, 1)

            def v_out(n, par):
                act.wait_ge(v_projected, n + 1)
                act.activation(v[par][:, :, :], aux_t, ACT.Copy).then_inc(v_ready, 1)

            def prepare(n, par):
                for step in (h_t, q_out, v_out):
                    step(n, par)

            table = {2: h_t, 3: q_out, 6: v_out}

            def exps(m, i):
                act.wait_ge(leaky, m + 1)
                act.wait_ge(shift_ready, m + 1)
                tile = z[:, i % 2, :]
                act.activation(tile, tile, ACT.Exp, bias=shift[:, i % 2:i % 2 + 1],
                               accum_out=total[:, i % KEEP:i % KEEP + 1]).then_inc(exp_done, 1)

            def low_half(m):
                act.wait_ge(turned, m + 1)
                act.activation(zt[:, 0:4, :], t_ps[:, 0, :].rearrange("p (t n) -> p t n", t=4), ACT.Copy).then_inc(zt_low, 1)

            def step(b, i, first):
                m = T * b + i
                if i < T:
                    exps(m, i)
                if not (first and i < 1):
                    low_half(m - 1)

            def stage(b, par, first, more):
                for i in range(T):
                    step(b, i, first)
                    if more and i in table:
                        table[i](b + 1, 1 - par)

            walk(act, prepare, stage, lambda: step(B - 1, T, False))

        @block.vector
        def _(dve):
            def stats(n, par):
                nm.dve_stats(dve, n)
                nm.dve_moments(dve, n)

            def scale(n, par):
                nm.dve_scale(dve, n, par)
                nm.dve_relu(dve, n, par)

            def k_out(n, par):
                dve.wait_ge(k_projected, n + 1)
                dve.tensor_copy(k[par][:, :], aux[:, :]).then_inc(k_ready, 1)

            def prepare(n, par):
                for step in (stats, scale, k_out):
                    step(n, par)
                for t in range(T):
                    dve.wait_ge(adj_loaded[t % 2], 16 * (t // 2 + 1))
                    dve.tensor_scalar(bias[:, t, :], adj_in[:, t % 2, :], 0, NEG, ALU.is_le,
                                      ALU.mult).then_inc(adj_used, 1)
                dve.wait_ge(adj_used, T)

            table = {0: stats, 1: scale, 4: k_out}

            def mask(m, i):
                a = i % 2
                wait_apart(c, dve, s_ready, m + 1)
                dve.tensor_tensor_reduce(z[:, a, :], s_ps[:, :], bias[:, i, :], 1.0, -3.0e38, ALU.add, ALU.max,
                                         top[:, a:a + 1]).then_inc(biased, 1)
                dve.wait_ge(biased, m + 1)
                dve.tensor_scalar(minus[:, a:a + 1], top[:, a:a + 1], -1.0, None, ALU.mult).then_inc(minus_ready, 1)
                dve.scalar_tensor_tensor(out=z[:, a, :], in0=z[:, a, :], scalar=0.2, in1=z[:, a, :], op0=ALU.mult,
                                         op1=ALU.max).then_inc(leaky, 1)
                dve.wait_ge(minus_ready, m + 1)
                dve.scalar_tensor_tensor(out=shift[:, a:a + 1], in0=top[:, a:a + 1], scalar=-0.2,
                                         in1=minus[:, a:a + 1], op0=ALU.mult, op1=ALU.min).then_inc(shift_ready, 1)

            def high_half(m):
                dve.wait_ge(turned, m + 1)
                dve.tensor_copy(zt[:, 4:8, :], t_ps[:, 1, :].rearrange("p (t n) -> p t n", t=4)).then_inc(zt_high, 1)

            def output(m, b, i):
                a = i % KEEP
                dve.reciprocal(inv[:, a:a + 1], total[:, a:a + 1]).then_inc(inverted, 1)
                dve.wait_ge(inverted, m + 1)
                dve.wait_ge(o_ready, m + 1)
                dve.tensor_scalar(res[:, :], o_ps[:, i % 2, 0:F], inv[:, a:a + 1], 0.0, ALU.mult,
                                  ALU.max).then_inc(res_ready, 1)
                dve.wait_ge(res_ready, m + 1)
                xt = c.x[:, b, i, :]
                dve.tensor_tensor(xt, xt, res[:, :], ALU.add).then_inc(x_updated, 1)

            def step(b, i, first):
                m = T * b + i
                if i < T:
                    mask(m, i)
                if not (first and i < 1) and i < T + 1:
                    high_half(m - 1)
                if not (first and i < 2):
                    output(m - 2, b if i >= 2 else b - 1, (i - 2) % T)

            def stage(b, par, first, more):
                for i in range(T):
                    if more and i in table and i < 4:
                        table[i](b + 1, 1 - par)
                    step(b, i, first)
                    if more and i == 4:
                        table[i](b + 1, 1 - par)

            def tail():
                step(B - 1, T, False)
                step(B - 1, T + 1, False)

            walk(dve, prepare, stage, tail)


def build(nc, a, out, layers=(0, 1, 2, 3)):
    with ExitStack() as ctx:
        c = Core(nc, ctx)
        if 0 in layers:
            layer0(c, a["x"], a["adj_t"], a)
        c.edge = c.sb("edge", [P, T, N], BF16)
        if 1 in layers:
            additive_layer(c, 1, 4, {"wv": a["w_1"], "a": (a["a_1"][0:F], a["a_1"][F:2 * F]),
                                     "adj_t": a["adj_t"]})
        if 2 in layers:
            additive_layer(c, 2, 8, {"wv": a["w_2"], "a": (a["a_src"], a["a_dst"]), "w_out_t": a["w_out_t"],
                                     "beta_tilde": a["beta_tilde"]})
        if 3 in layers:
            layer3(c, out, a["adj"], a)
            return
        done = c.sem("out_stored")
        with nc.Block() as block:
            @block.sync
            def _(sp):
                for b in range(B):
                    sp.dma_start(out[b].rearrange("(t p) f -> p t f", p=P), c.x[:, b, :, :]).then_inc(done, 16)
                sp.wait_ge(done, 16 * B)


def layouts(x, adj, L0_gnn_Wq, L0_gnn_bq, L0_gnn_Wk, L0_gnn_bk, L0_gnn_Wv, L0_gnn_bv, L0_gnn_Wo, L0_gnn_bo,
            L0_gnn_gamma, L0_gnn_beta, L1_gnn_W, L1_gnn_a, L2_gnn_W, L2_gnn_a_src, L2_gnn_a_dst,
            L2_gnn_beta_tilde, L2_gnn_W_out, L3_gnn_W1, L3_gnn_W2, L3_gnn_W3):
    import numpy as _np

    k, m, j = _np.ogrid[0:P, 0:P, 0:T]
    return {
        "pick": _np.ascontiguousarray(_np.broadcast_to(m[:, 0:32].transpose(0, 2, 1) % T == j.transpose(0, 2, 1),
                                                       (P, T, 32)), _np.float32),
        "spread": _np.ascontiguousarray((k == 32 * (m // 32) + j).transpose(0, 2, 1), _np.float32),
        "x": x, "adj": adj, "adj_t": adj.T,
        "wq_t": L0_gnn_Wq.T, "wk_t": L0_gnn_Wk.T, "wv_t": L0_gnn_Wv.T, "wo_t": L0_gnn_Wo.T,
        "bq": L0_gnn_bq.reshape(F, 1), "bk": L0_gnn_bk.reshape(F, 1), "bv": L0_gnn_bv, "bo": L0_gnn_bo,
        "gamma": L0_gnn_gamma, "beta": L0_gnn_beta,
        "w_1": L1_gnn_W.transpose(1, 0, 2).reshape(F, F),
        "a_1": L1_gnn_a.reshape(4, 2, F // 4).transpose(1, 0, 2).reshape(2 * F),
        "w_2": L2_gnn_W.transpose(1, 0, 2).reshape(F, F),
        "a_src": L2_gnn_a_src.reshape(F), "a_dst": L2_gnn_a_dst.reshape(F),
        "beta_tilde": L2_gnn_beta_tilde.reshape(1), "w_out_t": L2_gnn_W_out.T,
        "w1": L3_gnn_W1, "w2": L3_gnn_W2, "w3": L3_gnn_W3,
    }


def kernel(**inputs):
    import numpy as _np
    import concourse.bacc as _bacc
    from concourse import mybir as _mybir
    from concourse.bass_utils import run_bass_kernel_spmd as _run

    nc = _bacc.Bacc("TRN2", target_bir_lowering=False, num_devices=1)
    arrays = {f"in_{k}": _np.ascontiguousarray(v) for k, v in layouts(**inputs).items()}
    args = {k[3:]: nc.dram_tensor(k, v.shape, _mybir.dt.from_np(v.dtype), kind="ExternalInput").ap()
            for k, v in arrays.items()}
    out = nc.dram_tensor("out_x", (B, N, F), F32, kind="ExternalOutput").ap()
    build(nc, args, out)
    return _run(nc, [arrays], core_ids=[0]).results[0]["out_x"]
```

```python
from contextlib import ExitStack

import concourse.bass as bass
from concourse import mybir

F32 = mybir.dt.float32
F32R = mybir.dt.float32r
BF16 = mybir.dt.bfloat16
I32 = mybir.dt.int32
ALU = mybir.AluOpType
ACT = mybir.ActivationFunctionType
AX = mybir.AxisListType
RMAX = bass.bass_isa.ReduceOp.max
RADD = bass.bass_isa.ReduceOp.add

P = 128
B, N, F = 8, 1024, 128
T = N // P
HALF = 512
EPS = 1e-5
CLIP_LO, CLIP_HI = 4.5399929762484854e-05, 22026.465794806718
STEEP = 2.0 ** 60
NEG = -1.0e30
HEADS = {1: 4, 2: 8}
MAX_SPREAD = 60.0


class Core:

    def __init__(self, nc, ctx):
        self.nc = nc
        self.ctx = ctx
        sb = self.sb
        self.x = sb("x", [P, B, T, F], F32)
        self.h = sb("h", [P, 2, T, F], F32)
        self.h_t = sb("h_t", [P, N], F32)
        self.ident = sb("ident", [P, P], F32)
        self.ones = sb("ones", [P, 1], F32)
        self.mhalf = sb("mhalf", [P, T], F32)
        self.stats = sb("stats", [P, T, 6], F32)
        self.moments = sb("moments", [P, T, 2], F32)
        self.var_eps = sb("var_eps", [P, T], F32)
        self.rstd = sb("rstd", [P, T], F32)
        self.minus_mean = sb("minus_mean", [P, T], F32)
        self.offset = sb("offset", [P, T], F32)
        self.wa = {n: sb(f"wa{n}", [P, 2, heads], F32) for n, heads in HEADS.items()}
        self.wide = sb("wide", [P, 2], I32)
        self.prior = sb("prior", [P, 1], F32)
        self.passed = self.sem("passed")
        self.norm_sems = [self.sem(name) for name in ("stats_done", "moments_done", "var_done", "rstd_done",
                                                      "offset_done", "h_ready", "h_turned", "h_t_ready")]

    def sb(self, name, shape, dt, ctx=None):
        return (ctx or self.ctx).enter_context(self.nc.sbuf_tensor(name, shape, dt))

    def ps(self, name, shape, ctx):
        return ctx.enter_context(self.nc.psum_tensor(name, shape, F32))

    def sem(self, name):
        return self.ctx.enter_context(self.nc.semaphore(name))


class Norm:

    def __init__(self, c, layer, aux):
        self.c, self.aux, self.layer = c, aux, layer
        (self.stats_done, self.moments_done, self.var_done, self.rstd_done, self.offset_done, self.h_ready,
         self.h_turned, self.h_t_ready) = c.norm_sems

    def upto(self, n):
        return n + B * self.layer + 1

    def dve_stats(self, eng, n):
        c = self.c
        for t in range(T):
            ins = eng.bn_stats(c.stats[:, t, :], c.x[:, n, t, :])
        ins.then_inc(self.stats_done, 1)

    def dve_moments(self, eng, n):
        c = self.c
        wait_apart(self.c, eng, self.stats_done, self.upto(n))
        for t in range(T):
            ins = eng.bn_aggr(c.moments[:, t, :], c.stats[:, t, :])
        ins.then_inc(self.moments_done, 1)
        eng.wait_ge(self.moments_done, self.upto(n))
        eng.tensor_scalar(c.minus_mean[:, :], c.moments[:, :, 0], -1.0, None, ALU.mult)
        eng.tensor_scalar(c.var_eps[:, :], c.moments[:, :, 1], EPS, None, ALU.add).then_inc(self.var_done, 1)

    def pool_rstd(self, eng, n):
        c = self.c
        eng.wait_ge(self.var_done, self.upto(n))
        eng.tensor_tensor(c.rstd[:, :], c.var_eps[:, :], c.mhalf[:, :], ALU.pow).then_inc(self.rstd_done, 1)
        eng.wait_ge(self.rstd_done, self.upto(n))
        eng.tensor_tensor(c.offset[:, :], c.minus_mean[:, :], c.rstd[:, :], ALU.mult).then_inc(self.offset_done, 1)

    def act_h(self, eng, n, par):
        c = self.c
        eng.wait_ge(self.offset_done, self.upto(n))
        for t in range(T):
            ins = eng.activation(c.h[:, par, t, :], c.x[:, n, t, :], ACT.Relu, bias=c.offset[:, t:t + 1],
                                 scale=c.rstd[:, t:t + 1])
        ins.then_inc(self.h_ready, 1)

    def pe_turn(self, eng, n, par):
        c = self.c
        eng.wait_ge(self.h_ready, self.upto(n))
        for t in range(T):
            ins = eng.transpose(self.aux[:, t * P:(t + 1) * P], c.h[:, par, t, :], c.ident[:, :])
        ins.then_inc(self.h_turned, 1)

    def act_h_t(self, eng, n):
        eng.wait_ge(self.h_turned, self.upto(n))
        eng.activation(self.c.h_t[:, :], self.aux[:, :], ACT.Copy).then_inc(self.h_t_ready, 1)


def wait_apart(c, eng, sem, value):
    eng.wait_ge(sem, value)
    eng.sem_inc(c.passed, 1)


def walk(eng, prepare, stage, tail=lambda: None):
    prepare(0, 0)
    stage(0, 0, True, True)
    stage(1, 1, False, True)
    with eng.Fori(1, B // 2 - 1) as pair:
        stage(2 * pair, 0, False, True)
        stage(2 * pair + 1, 1, False, True)
    stage(B - 2, 0, False, True)
    stage(B - 1, 1, False, False)
    tail()


def project_nodes(eng, out, h_t, w):
    for t in range(T):
        ins = eng.matmul(out[:, t, :], h_t[:, t * P:(t + 1) * P], w, start=True, stop=True)
    return ins


def project_rows(eng, out, w, h_t):
    for i in range(2):
        ins = eng.matmul(out[:, i * HALF:(i + 1) * HALF], w, h_t[:, i * HALF:(i + 1) * HALF],
                         start=True, stop=True)
    return ins


def layer0(c, x_in, adj_t, w):
    nc = c.nc
    H, DH = 4, F // 4
    STEPS = 2 * T
    COPIES = 4
    STACK = 16 * COPIES * H
    SCALE = float(DH) ** -0.5
    with ExitStack() as ctx:
        sb = lambda name, shape, dt=F32: c.sb(name, shape, dt, ctx)
        bound = sb("bound", [P, T, N])
        chunk = sb("chunk", [P, T, HALF])
        pick = sb("pick", [P, T, 32])
        spread = sb("spread", [P, T, P])
        wq, wk, wv, wo = (sb(k, [P, F]) for k in ("wq", "wk", "wv", "wo"))
        bq, bk = sb("bq", [P, 1]), sb("bk", [P, 1])
        bv, bo, gamma, beta = (sb(k, [P, F]) for k in ("bv", "bo", "gamma", "beta"))
        square, norm, widest = (sb(k, [P, 12]) for k in ("square", "norm", "widest"))
        pr = sb("pr", [P, 8])
        split = sb("split", [P, 2, N], F32R)
        qs = [sb(f"qs{i}", [P, H, N], F32R) for i in range(2)]
        ks = [sb(f"ks{i}", [P, H, N], F32R) for i in range(2)]
        v = [sb(f"v{i}", [P, T, F]) for i in range(2)]
        w_add, a_add = v[1][:, 0:2, :], v[1][:, 2:6, :]
        e = sb("e", [P, 4, 2, HALF])
        adj_in = [chunk[:, :, :].rearrange("p (t a) n -> p t (a n)", t=4).bitcast(I32),
                  e[:, :, :, :].rearrange("p t a n -> p t (a n)").bitcast(I32)]
        inv_sum = sb("inv_sum", [P, HALF])
        ctx_sb = sb("ctx_sb", [P, 2, HALF])
        late = sb("late", [P, 4, F])
        u = c.h_t[:, 0:HALF].rearrange("p (t f) -> p t f", t=4)
        stats2, moments2 = sb("stats2", [P, 4, 6]), sb("moments2", [P, 4, 2])
        var2, rstd2 = sb("var2", [P, 4]), sb("rstd2", [P, 4])
        s_ps = c.ps("s_ps", [P, 2, 2, HALF], ctx)
        ctx_ps = c.ps("ctx_ps", [P, HALF], ctx)
        sum_ps = c.ps("sum_ps", [P, HALF], ctx)
        aux = c.ps("aux0", [P, N], ctx)
        aux_t = aux[:, :].rearrange("p (t f) -> p t f", t=T)

        loaded = c.sem("weights0_loaded")
        x_loaded = [c.sem(f"x_loaded_{k}") for k in ("0", "1", "2_on")]
        adj_loaded, bounded_above = [c.sem("adj_loaded_a"), c.sem("adj_loaded_b")], c.sem("bounded_above")
        bounded, consts, ident0 = c.sem("bounded"), c.sem("consts"), c.sem("ident_zeroed")
        nm = Norm(c, 0, aux)
        q_projected, q_hi, q_split, q_stacked = (c.sem(f"q_{k}") for k in ("projected", "hi", "split", "stacked"))
        k_projected, k_hi, k_split, k_stacked = (c.sem(f"k_{k}") for k in ("projected", "hi", "split", "stacked"))
        v_projected, v_ready, h_biased = c.sem("v_projected"), c.sem("v_ready"), c.sem("h_biased")
        s_ready, exp_done, p_ready, pv_done = (c.sem(k) for k in ("s_ready", "exp_done", "p_ready", "pv_done"))
        summed, inverted, chunk_copied, inv_spread, chunk_weighed, added, late_biased = (
            c.sem(k) for k in ("summed", "inverted", "chunk_copied", "inv_spread", "chunk_weighed", "added",
                               "late_biased"))
        o_projected, u_ready = c.sem("o_projected"), c.sem("u_ready")
        stats2_done, moments2_done, var2_done, rstd2_done, u_scaled, x_updated = (
            c.sem(k) for k in ("stats2_done", "moments2_done", "var2_done", "rstd2_done", "u_scaled", "x_updated0"))
        add_loaded, add_mult, wa_squared, wa_norms, prior_steps, prior_ready = (
            c.sem(k) for k in ("add_loaded", "add_mult", "wa_squared", "wa_norms", "prior_steps", "prior_ready"))
        block = ctx.enter_context(nc.Block())

        def weighed_at(i):
            return int(1 <= i <= 8), (i - 1) % T

        @block.sync
        def _(sp):
            def load_x(b, done):
                sp.dma_start(c.x[:, b, :, :], x_in[b].rearrange("(t p) f -> p t f", p=P)).then_inc(done, 16)

            load_x(0, x_loaded[0])
            for dst, name in ((wq, "wq_t"), (wk, "wk_t"), (wv, "wv_t"), (wo, "wo_t"), (bq, "bq"), (bk, "bk")):
                sp.dma_start(dst[:, :], w[name]).then_inc(loaded, 16)
            for dst, name in ((bv, "bv"), (bo, "bo"), (gamma, "gamma"), (beta, "beta")):
                sp.dma_start(dst[:, :], w[name].partition_broadcast(P)).then_inc(loaded, 16)
            sp.dma_start(pick[:, :, :], w["pick"]).then_inc(loaded, 16)
            sp.dma_start(spread[:, :, :], w["spread"]).then_inc(loaded, 16)
            for n in HEADS:
                sp.dma_start(w_add[:, n - 1, :], w[f"w_{n}"]).then_inc(add_loaded, 16)
                for k in range(2):
                    sp.dma_start(a_add[:, 2 * (n - 1) + k, :],
                                 w[f"a_{n}"][k * F:(k + 1) * F].partition_broadcast(P)).then_inc(add_loaded, 16)
            sp.dma_start(pr[:, 0:1], w["beta_tilde"].partition_broadcast(P)).then_inc(add_loaded, 16)
            for t in range(T):
                sp.dma_start(adj_in[t // 4][:, t % 4, :], adj_t[t * P:(t + 1) * P, :]).then_inc(adj_loaded[t // 4], 16)
            for b in range(1, B):
                load_x(b, x_loaded[min(b, 2)])

            def stack(n, par, dst, parts, split_done, stacked):
                sp.wait_ge(split_done, n + 1)
                for copy in range(COPIES):
                    for h in range(H):
                        sp.dma_start(dst[par][copy * DH:(copy + 1) * DH, h, :].bitcast(F32),
                                     split[h * DH:(h + 1) * DH, parts[copy], :].bitcast(F32)).then_inc(stacked, 16)

            def prepare(n, par):
                wait_apart(c, sp, s_ready, 32 * n + 32)
                stack(n, par, qs, (0, 0, 1, 1), q_split, q_stacked)
                stack(n, par, ks, (0, 1, 0, 1), k_split, k_stacked)

            def stage(b, par, first, more):
                if more:
                    prepare(b + 1, 1 - par)

            walk(sp, prepare, stage)

        @block.gpsimd
        def _(pool):
            pool.memset(c.ident[:, :], 0.0).then_inc(ident0, 1)
            pool.memset(c.ones[:, :], 1.0)
            pool.memset(c.mhalf[:, :], -0.5)
            pool.wait_ge(ident0, 1)
            pool.affine_select(out=c.ident[:, :], in_=c.ident[:, :], compare_op=ALU.not_equal, fill=1.0, base=0,
                               pattern=[[-1, P]], channel_multiplier=1).then_inc(consts, 1)
            pool.wait_ge(consts, 1)
            pool.wait_ge(loaded, 192)

            def bias(n, par):
                pool.wait_ge(nm.h_turned, nm.upto(n))
                h0 = c.h[:, par, 0:4, :]
                pool.tensor_tensor(h0, h0, bo[:, :].unsqueeze(1).to_broadcast([P, 4, F]),
                                   ALU.add).then_inc(h_biased, 1)

            def bias_late(n, par):
                pool.wait_ge(u_ready, 2 * n + 2)
                pool.tensor_tensor(late[:, :, :], c.h[:, par, 4:8, :], bo[:, :].unsqueeze(1).to_broadcast([P, 4, F]),
                                   ALU.add).then_inc(late_biased, 1)

            def prepare(n, par):
                nm.pool_rstd(pool, n)
                bias(n, par)
                pool.wait_ge(wa_squared, 1)
                pool.partition_all_reduce(norm[:, :], square[:, :], P, RADD).then_inc(wa_norms, 1)

            def rstd_out(b, half):
                pool.wait_ge(var2_done, 2 * b + half + 1)
                pool.tensor_tensor(rstd2[:, :], var2[:, :], c.mhalf[:, 0:4], ALU.pow).then_inc(rstd2_done, 1)

            def add(b, i):
                half, j = weighed_at(i)
                m = 2 * b + half - (0 if i >= 9 else 2)
                if j > 0:
                    pool.wait_ge(chunk_weighed, 8 * m + j + 9)
                    pool.wait_ge(added, 7 * m + j + 7)
                    acc = ctx_sb[:, half, :]
                    pool.tensor_tensor(acc, acc, chunk[:, j, :], ALU.add).then_inc(added, 1)

            def stage(b, par, first, more):
                for i in range(STEPS):
                    if not (first and i < 9):
                        add(b, i)
                    if more:
                        if i == 1:
                            nm.pool_rstd(pool, b + 1)
                        elif i == 8:
                            bias(b + 1, 1 - par)
                    if not first and i in (3, 15):
                        rstd_out(b - 1, int(i == 15))
                bias_late(b, par)

            def tail():
                for i in range(9):
                    add(B, i)
                    if i == 4:
                        rstd_out(B - 1, 0)
                rstd_out(B - 1, 1)

            pool.sem_inc(added, 8)
            walk(pool, prepare, stage, tail)

        @block.tensor
        def _(pe):
            pe.sem_inc(v_projected, 1)
            pe.sem_inc(s_ready, 64)
            pe.wait_ge(loaded, 192)
            pe.wait_ge(consts, 1)

            def turn(n, par):
                if not (isinstance(n, int) and n == 0):
                    pe.wait_ge(u_ready, 2 * n - 1)
                nm.pe_turn(pe, n, par)

            def q(n):
                pe.wait_ge(nm.h_t_ready, nm.upto(n))
                project_rows(pe, aux, wq[:, :], c.h_t).then_inc(q_projected, 1)

            def k(n):
                pe.wait_ge(q_split, n + 1)
                project_rows(pe, aux, wk[:, :], c.h_t).then_inc(k_projected, 1)

            def vv(n):
                pe.wait_ge(k_split, n + 1)
                project_nodes(pe, aux_t, c.h_t, wv[:, :]).then_inc(v_projected, 1)

            def prepare(n, par):
                turn(n, par)
                q(n)
                k(n)
                vv(n)

            def scores(b, par, i, hp):
                half, jt = divmod(i, T)
                pe.wait_ge(exp_done, 32 * b + 2 * i + hp + 1)
                for j in range(2):
                    ins = pe.matmul(s_ps[:, hp, j, :], ks[par][:, 2 * hp + j, jt * P:(jt + 1) * P],
                                    qs[par][:, 2 * hp + j, half * HALF:(half + 1) * HALF], start=True, stop=True)
                ins.then_inc(s_ready, 1)

            def sums(b, i):
                half, jt = divmod(i, T)
                pe.wait_ge(p_ready, 32 * b + 2 * i + 2)
                if jt == 0:
                    pe.wait_ge(inverted, 2 * b + half + 1)
                for h in range(H):
                    ins = pe.matmul(sum_ps[h * DH:(h + 1) * DH, :], pick[:, jt, :], e[:, 2 * (i % 2) + h // 2, h % 2, :],
                                    start=(jt == 0), stop=(jt == T - 1), tile_position=(0, h * DH))
                ins.then_inc(summed, 1)

            def spread_inverses(b, i):
                half, j = weighed_at(i)
                pe.wait_ge(inverted, 2 * b + half + (2 if i >= 9 else 0))
                pe.matmul(ctx_ps[:, :], spread[:, j, :], inv_sum[:, :], start=True, stop=True).then_inc(inv_spread, 1)

            def values(b, par, i):
                pe.wait_ge(chunk_copied, 16 * b + i + 1)
                pe.wait_ge(chunk_weighed, 16 * b + i + 1)
                for h in range(H):
                    ins = pe.matmul(ctx_ps[h * DH:(h + 1) * DH, :], v[par][:, i % T, h * DH:(h + 1) * DH],
                                    e[:, 2 * (i % 2) + h // 2, h % 2, :], start=True, stop=True,
                                    tile_position=(0, h * DH))
                ins.then_inc(pv_done, 1)

            def output(b, half):
                m = 2 * b + half
                pe.wait_ge(added, 7 * m + 15)
                pe.wait_ge(u_ready, m + 2)
                for t in range(4):
                    ins = pe.matmul(aux_t[:, t, :], ctx_sb[:, half, t * P:(t + 1) * P], wo[:, :], start=True, stop=True)
                ins.then_inc(o_projected, 1)

            def stacks(n):
                pe.wait_ge(q_stacked, STACK * (n + 1))
                pe.wait_ge(k_stacked, STACK * (n + 2))

            def stage(b, par, first, more):
                n = b + 1
                if first:
                    stacks(b)
                    for hp in range(2):
                        scores(b, par, 0, hp)
                    pe.wait_ge(v_ready, b + 1)
                for i in range(STEPS):
                    before = (b, par, i - 1) if i >= 1 else (b - 1, 1 - par, STEPS - 1)
                    after = (b, par, i + 1) if i + 1 < STEPS else (n, 1 - par, 0)
                    if not (first and i < 9):
                        pe.wait_ge(chunk_copied, 16 * b + i)
                        spread_inverses(b, i)
                    if not (first and i == 0):
                        sums(before[0], before[2])
                        values(*before)
                    if more or i + 1 < STEPS:
                        if i + 1 == STEPS:
                            stacks(n)
                        for hp in range(2):
                            scores(*after, hp)
                    if not first and i == 1:
                        output(b - 1, 0)
                    if more:
                        if i == 4:
                            turn(n, 1 - par)
                        elif i == 6:
                            q(n)
                        elif i == 8:
                            k(n)
                        elif i == 12:
                            vv(n)
                    if i == 14:
                        if more:
                            pe.wait_ge(v_ready, n + 1)
                        if not first:
                            output(b - 1, 1)

            def tail():
                sums(B - 1, STEPS - 1)
                pe.wait_ge(chunk_copied, 16 * B)
                spread_inverses(B, 0)
                values(B - 1, 1, STEPS - 1)
                for i in range(1, 9):
                    if i == 1:
                        pe.wait_ge(chunk_copied, 16 * B + 1)
                    else:
                        pe.wait_ge(chunk_weighed, 16 * B + i - 1)
                    spread_inverses(B, i)
                    if i == 2:
                        output(B - 1, 0)
                output(B - 1, 1)

            walk(pe, prepare, stage, tail)

        @block.scalar
        def _(act):
            act.sem_inc(exp_done, 2)
            act.sem_inc(chunk_copied, 1)
            act.sem_inc(k_stacked, STACK)
            act.wait_ge(loaded, 192)

            def h_t(n):
                act.wait_ge(v_projected, n + 1)
                if not (isinstance(n, int) and n == 0):
                    act.wait_ge(x_updated, 2 * n - 1)
                nm.act_h_t(act, n)

            def high(n, projected, bias, done, free, value):
                act.wait_ge(projected, n + 1)
                act.wait_ge(free, value)
                act.activation(split[:, 0, :], aux[:, :], ACT.Identity, bias=bias[:, 0:1]).then_inc(done, 1)

            def q(n):
                high(n, q_projected, bq, q_hi, k_stacked, STACK * (n + 1))

            def k(n):
                high(n, k_projected, bk, k_hi, q_stacked, STACK * (n + 1))

            def prepare(n, par):
                nm.act_h(act, n, par)
                h_t(n)
                q(n)
                k(n)
                act.wait_ge(prior_steps, 2)
                act.activation(pr[:, 3:4], pr[:, 2:3], ACT.Exp, scale=-1.0).then_inc(prior_ready, 1)
                act.wait_ge(prior_ready, 1)
                act.activation(pr[:, 4:5], pr[:, 3:4], ACT.Ln, bias=c.ones[:, 0:1])
                act.activation(pr[:, 6:7], c.ones[:, 0:1], ACT.Ln, bias=pr[:, 5:6]).then_inc(prior_ready, 1)
                act.wait_ge(bounded, 2)

            def exps(b, i, hp):
                act.wait_ge(s_ready, 32 * b + 2 * i + hp + 65)
                if hp == 0:
                    act.wait_ge(pv_done, 16 * b + i + 1)
                act.activation(e[:, 2 * (i % 2) + hp, :, :], s_ps[:, hp, :, :], ACT.Exp,
                               scale=SCALE).then_inc(exp_done, 1)

            def copy_chunk(b, i):
                act.wait_ge(pv_done, 16 * b + i + 3)
                act.wait_ge(added, 14 * b + 7 * (i // T) + i % T + 1)
                act.activation(chunk[:, i % T, :], ctx_ps[:, :], ACT.Copy).then_inc(chunk_copied, 1)

            def stage(b, par, first, more):
                n = b + 1
                for i in range(STEPS):
                    if i >= 2:
                        copy_chunk(b, i - 2)
                    elif not first:
                        copy_chunk(b - 1, i + STEPS - 2)
                    exps(b, i, 0)
                    exps(b, i, 1)
                    if more:
                        if i == 3:
                            if not first:
                                act.wait_ge(late_biased, b)
                                act.wait_ge(u_ready, 2 * b + 1)
                            nm.act_h(act, n, 1 - par)
                        elif i == 5:
                            h_t(n)
                        elif i == 7:
                            q(n)
                        elif i == 11:
                            k(n)

            def tail():
                copy_chunk(B - 1, STEPS - 2)
                copy_chunk(B - 1, STEPS - 1)

            act.sem_inc(pv_done, 2)
            walk(act, prepare, stage, tail)

        @block.vector
        def _(dve):
            dve.sem_inc(u_ready, 2)
            dve.sem_inc(x_updated, 2)
            dve.sem_inc(inverted, 1)
            dve.sem_inc(chunk_weighed, 8)
            dve.wait_ge(loaded, 192)
            dve.wait_ge(consts, 1)
            def additive_weights():
                dve.wait_ge(add_loaded, 16 * 7)
                for n in HEADS:
                    for k in range(2):
                        a = a_add[:, 2 * (n - 1) + k, :]
                        dve.tensor_tensor(a, a, w_add[:, n - 1, :], ALU.mult)
                dve.memset(pr[:, 5:6], 1e-6)
                dve.tensor_scalar(pr[:, 1:2], pr[:, 0:1], -1.0, None, ALU.mult).then_inc(add_mult, 1)
                dve.wait_ge(add_mult, 1)
                for n, heads in HEADS.items():
                    dve.tensor_reduce(c.wa[n][:, :, :], a_add[:, 2 * n - 2:2 * n, :].rearrange("p k (h d) -> p k h d", h=heads),
                                      AX.X, ALU.add)
                dve.tensor_tensor(pr[:, 2:3], pr[:, 0:1], pr[:, 1:2], ALU.max).then_inc(prior_steps, 2)
                dve.wait_ge(prior_steps, 2)
                for at, n in ((0, 1), (4, 2)):
                    d = c.wa[n][:, 1, :]
                    ins = dve.tensor_tensor(square[:, at:at + HEADS[n]], d, d, ALU.mult)
                ins.then_inc(wa_squared, 1)

            def finish_additive_weights():
                dve.wait_ge(prior_ready, 2)
                dve.scalar_tensor_tensor(out=pr[:, 7:8], in0=pr[:, 0:1], scalar=0.0, in1=pr[:, 4:5], op0=ALU.max,
                                         op1=ALU.add)
                dve.wait_ge(wa_norms, 1)
                for i, at in enumerate((0, 4)):
                    ins = dve.tensor_reduce(widest[:, i:i + 1], norm[:, at:at + 4 * (i + 1)], AX.X, ALU.max)
                ins.then_inc(prior_steps, 1)
                dve.wait_ge(prior_steps, 3)
                dve.tensor_tensor(c.prior[:, :], pr[:, 7:8], pr[:, 6:7], ALU.mult)
                dve.tensor_scalar(c.wide[:, :], widest[:, 0:2], MAX_SPREAD ** 2 / (2 * F), None, ALU.is_gt)

            def bounds(part):
                dve.wait_ge(adj_loaded[part], 64)
                some = bound[:, 4 * part:4 * part + 4, :]
                dve.tensor_scalar(some, adj_in[part], 0, CLIP_HI, ALU.not_equal, ALU.mult).then_inc(bounded_above, 1)
                dve.wait_ge(bounded_above, part + 1)
                dve.tensor_scalar(some, some, CLIP_LO, None, ALU.max).then_inc(bounded, 1)

            def low(n, hi_done, bias, done):
                dve.wait_ge(hi_done, n + 1)
                dve.scalar_tensor_tensor(out=split[:, 1, :], in0=aux[:, :], scalar=bias[:, 0:1],
                                         in1=split[:, 0, :].bitcast(F32), op0=ALU.add,
                                         op1=ALU.subtract).then_inc(done, 1)

            def v_out(n, par):
                dve.wait_ge(v_projected, n + 2)
                for half in range(2):
                    sl = slice(4 * half, 4 * half + 4)
                    ins = dve.tensor_tensor(v[par][:, sl, :], aux_t[:, sl, :],
                                            bv[:, :].unsqueeze(1).to_broadcast([P, 4, F]), ALU.add)
                ins.then_inc(v_ready, 1)

            def prepare(n, par):
                dve.wait_ge(x_loaded[0], 16)
                nm.dve_stats(dve, n)
                nm.dve_moments(dve, n)
                low(n, q_hi, bq, q_split)
                low(n, k_hi, bk, k_split)
                v_out(n, par)
                additive_weights()
                bounds(0)
                bounds(1)
                finish_additive_weights()
                dve.wait_ge(bounded, 2)

            def clip(b, i, hp):
                half, jt = divmod(i, T)
                dve.wait_ge(exp_done, 32 * b + 2 * i + hp + 3)
                tile = e[:, 2 * (i % 2) + hp, :, :]
                lim = bound[:, jt, half * HALF:(half + 1) * HALF].unsqueeze(1).to_broadcast([P, 2, HALF])
                dve.scalar_tensor_tensor(out=tile, in0=tile, scalar=CLIP_LO, in1=lim, op0=ALU.max,
                                         op1=ALU.min).then_inc(p_ready, 1)

            def invert(b, half):
                dve.wait_ge(summed, 16 * b + 8 * half + 8)
                dve.reciprocal(inv_sum[:, :], sum_ps[:, :]).then_inc(inverted, 1)

            def weigh(b, i):
                half, j = weighed_at(i)
                m = 2 * b + half - (0 if i >= 9 else 2)
                dve.wait_ge(inv_spread, 8 * m + j + 1)
                values = chunk[:, j, :]
                dve.tensor_tensor(ctx_sb[:, half, :] if j == 0 else values, values, ctx_ps[:, :],
                                  ALU.mult).then_inc(chunk_weighed, 1)

            def residual(b, par, half):
                m = 2 * b + half
                dve.wait_ge(o_projected, m + 1)
                dve.wait_ge(late_biased if half else h_biased, b + 1)
                dve.tensor_tensor(u[:, :, :], aux_t[:, 0:4, :], late[:, :, :] if half else c.h[:, par, 0:4, :],
                                  ALU.add).then_inc(u_ready, 1)
                dve.wait_ge(u_ready, m + 3)
                for t in range(4):
                    ins = dve.bn_stats(stats2[:, t, :], u[:, t, :])
                ins.then_inc(stats2_done, 1)
                wait_apart(c, dve, stats2_done, m + 1)
                for t in range(4):
                    ins = dve.bn_aggr(moments2[:, t, :], stats2[:, t, :])
                ins.then_inc(moments2_done, 1)
                dve.wait_ge(moments2_done, m + 1)
                dve.tensor_scalar(var2[:, :], moments2[:, :, 1], EPS, None, ALU.add).then_inc(var2_done, 1)

            def update(b, half):
                m = 2 * b + half
                dve.wait_ge(rstd2_done, m + 1)
                for t in range(4):
                    ins = dve.scalar_tensor_tensor(out=u[:, t, :], in0=u[:, t, :], scalar=moments2[:, t, 0:1],
                                                   in1=gamma[:, :], op0=ALU.subtract, op1=ALU.mult)
                    xt = c.x[:, b, 4 * half + t, :]
                    ins = dve.tensor_tensor(xt, xt, beta[:, :], ALU.add)
                ins.then_inc(u_scaled, 1)
                dve.wait_ge(u_scaled, m + 1)
                for t in range(4):
                    xt = c.x[:, b, 4 * half + t, :]
                    ins = dve.scalar_tensor_tensor(out=xt, in0=u[:, t, :], scalar=rstd2[:, t:t + 1], in1=xt,
                                                   op0=ALU.mult, op1=ALU.add)
                ins.then_inc(x_updated, 1)
                dve.wait_ge(x_updated, m + 3)

            def stage(b, par, first, more):
                n = b + 1
                if first:
                    dve.wait_ge(x_loaded[1], 16)
                elif isinstance(b, int) and b == 1:
                    dve.wait_ge(x_loaded[2], 16 * (B - 2))
                for i in range(STEPS):
                    if not (first and i < 9):
                        weigh(b, i)
                    clip(b, i, 0)
                    if i == 8:
                        invert(b, 0)
                    elif i == 0 and not first:
                        invert(b - 1, 1)
                    clip(b, i, 1)
                    if not first:
                        if i == 2:
                            residual(b - 1, 1 - par, 0)
                        elif i == 4:
                            update(b - 1, 0)
                        elif i == 14:
                            residual(b - 1, 1 - par, 1)
                        elif i == 15:
                            update(b - 1, 1)
                    if more:
                        if i == 0:
                            nm.dve_stats(dve, n)
                        elif i == 1:
                            nm.dve_moments(dve, n)
                        elif i == 7:
                            low(n, q_hi, bq, q_split)
                        elif i == 11:
                            low(n, k_hi, bk, k_split)
                        elif i == 13:
                            v_out(n, 1 - par)

            def tail():
                for i in range(9):
                    weigh(B, i)
                    if i == 0:
                        invert(B - 1, 1)
                    elif i == 4:
                        residual(B - 1, 1, 0)
                        update(B - 1, 0)
                residual(B - 1, 1, 1)
                update(B - 1, 1)

            walk(dve, prepare, stage, tail)


def additive_layer(c, layer, w):
    nc = c.nc
    H = HEADS[layer]
    DH = F // H
    W1 = DH + 1
    NC = 2 * W1
    NS = 3 * NC
    OWN = 2
    SC = T - OWN
    RING = 4
    L = str(layer)
    with ExitStack() as ctx:
        sb = lambda name, shape, dt=F32: c.sb(name + L, shape, dt, ctx)
        wv = sb("wv", [P, F])
        wa = c.wa[layer]
        wh = sb("wh", [P, T, H, DH])
        sd = sb("sd", [P, T, 2, H])
        s_row = sb("s_row", [H, N])
        top_part, top = sb("top_part", [P, H]), sb("top", [P, H])
        z, dz = sb("z", [P, T, H]), sb("dz", [P, T, H])
        z_up, z_down = sb("z_up", [P, T, H]), sb("z_down", [P, T, H])
        up = [sb(f"up{i}_", [P, T, H]) for i in range(2)]
        down = [sb(f"down{i}_", [P, T, H]) for i in range(2)]
        keyf = sb("keyf", [P, T, H, 2])
        steep_d = [sb(f"steep_d{i}_", [P, T, H]) for i in range(2)]
        minus_d = [sb(f"minus_d{i}_", [P, T, H]) for i in range(2)]
        vals = sb("vals", [P, T, H, 2, W1])
        parts = [sb(f"parts{i}_", [P, T, H, 3, 2, W1], BF16) for i in range(2)]
        s_all = sb("s_all", [P, 2, N])
        steep = sb("steep", [P, 4, N], BF16)
        g = [sb(f"g{i}_", [P, T, N], BF16) for i in range(2)]
        sums = [sb(f"sums{i}_", [P, H, T, 2, W1]) for i in range(2)]
        base = [sb(f"base{i}_", [P, T, H, W1]) for i in range(2)]
        inv = sb("inv", [P, H, T])
        out = sb("out", [P, T, F])
        neg = sb("neg", [P, T, F])
        acc = c.ps("acc" + L, [P, 4, HALF], ctx)
        post = c.ps("post" + L, [P, 2, HALF], ctx)
        aux = c.ps("aux" + L, [P, N], ctx)
        aux_t = aux[:, :].rearrange("p (t f) -> p t f", t=T)
        s_dram = c.nc.dram_tensor("s_rows" + L, (2, H, N), F32, kind="Internal").ap()
        if layer == 2:
            w_out = sb("w_out", [P, F])
            out_t = sb("out_t", [P, N])
            post_t = post[:, :, :].rearrange("p a (t f) -> p (a t) f", f=F)

        sems = []

        def sem(name):
            sems.append(c.sem(name + L))
            return sems[-1]

        nm = Norm(c, layer, aux)
        if layer == 1:
            adj_in = [m[:, :, :].rearrange("p t n -> p (t n)").bitcast(I32).rearrange("p (t n) -> p t n", t=4)
                      for m in g]
            adj_loaded, edge_ready = sem("adj_loaded"), sem("edge_ready")
        loaded = sem("loaded")
        v_projected, wh_ready, sd_projected, sd_ready, row_projected, row_ready = (
            sem(k) for k in ("v_projected", "wh_ready", "sd_projected", "sd_ready", "row_projected", "row_ready"))
        row_stored, s_loaded = sem("row_stored"), [sem("s_loaded_a"), sem("s_loaded_b")]
        top_partial, top_ready, z_ready, z_parts, factors = (
            sem(k) for k in ("top_partial", "top_ready", "z_ready", "z_parts", "factors"))
        vals_ready, hi_ready, rest1, mid_ready, parts_ready = (
            sem(k) for k in ("vals_ready", "hi_ready", "rest1", "mid_ready", "parts_ready"))
        base_summed, base_ready = sem("base_summed"), sem("base_ready")
        steep_ready, g_ready, acc_summed, acc_read = (
            sem(k) for k in ("steep_ready", "g_ready", "acc_summed", "acc_read"))
        scaled_sums, downs, totals, inverted, out_ready = (
            sem(k) for k in ("scaled_sums", "downs", "totals", "inverted", "out_ready"))
        x_updated = sem("x_updated")
        if layer == 1:
            neg_ready, exp_ready, x_relu = (sem(k) for k in ("neg_ready", "exp_ready", "x_relu"))
        else:
            out_turned, out_t_ready, out_projected = (
                sem(k) for k in ("out_turned", "out_t_ready", "out_projected"))
        block = ctx.enter_context(nc.Block())

        def part(par, k):
            return parts[par][:, :, :, k, :, :].rearrange("p t h k c -> p (t h) (k c)")

        def all_vals():
            return vals[:, :, :, :, :].rearrange("p t h k c -> p (t h) (k c)")

        def pieces(table, slot, n, par):
            for step in table.get(slot, ()):
                step(n, par)

        @block.sync
        def _(sp):
            sp.dma_start(wv[:, :], w["wv"]).then_inc(loaded, 16)
            if layer == 2:
                sp.dma_start(w_out[:, :], w["w_out_t"]).then_inc(loaded, 16)
            if layer == 1:
                for t in range(T):
                    sp.dma_start(adj_in[t // 4][:, t % 4, :], w["adj_t"][t * P:(t + 1) * P, :]).then_inc(adj_loaded, 16)
            sp.sem_inc(row_stored, 16)

            def prepare(n, par):
                sp.wait_ge(row_ready, n + 2)
                sp.dma_start(s_dram[par], s_row[:, :]).then_inc(row_stored, 16)

            def stage(b, par, first, more):
                sp.wait_ge(row_stored, 16 * b + 32)
                for h in range(H):
                    if more and H == 8 and h == H - 1:
                        prepare(b + 1, 1 - par)
                    sp.wait_ge(g_ready, T * (H * b + h) + T)
                    sp.dma_start(s_all[:, h % 2, :], s_dram[par, h, :].partition_broadcast(P)).then_inc(s_loaded[h % 2], 16)
                if more and H == 4:
                    prepare(b + 1, 1 - par)

            walk(sp, prepare, stage, lambda: None)

        @block.gpsimd
        def _(pool):
            def prepare_parts(n, par):
                wait_apart(c, pool, top_partial, n + 1)
                pool.partition_all_reduce(top[:, :], top_part[:, :], P, RMAX).then_inc(top_ready, 1)
                pool.wait_ge(hi_ready, n + 1)
                pool.tensor_tensor(all_vals(), all_vals(), part(par, 0), ALU.subtract).then_inc(rest1, 1)
                pool.wait_ge(mid_ready, n + 1)
                pool.tensor_tensor(part(par, 2), all_vals(), part(par, 1), ALU.subtract).then_inc(parts_ready, 1)

            def prepare(n, par):
                nm.pool_rstd(pool, n)
                prepare_parts(n, par)

            def combine(b, par):
                pool.wait_ge(acc_read, 4 * H * (b + 1) + 4)
                pool.wait_ge(base_ready, T * (b + 1))
                sm = sums[par]
                for h in range(H):
                    pool.tensor_tensor(sm[:, h, :, 0, :], sm[:, h, :, 0, :],
                                       up[par][:, :, h].unsqueeze(2).to_broadcast([P, T, W1]), ALU.mult)
                    ins = pool.tensor_tensor(sm[:, h, :, 1, :], base[par][:, :, h, :], sm[:, h, :, 1, :], ALU.subtract)
                ins.then_inc(scaled_sums, 1)
                pool.wait_ge(scaled_sums, b + 1)
                for h in range(H):
                    ins = pool.tensor_tensor(sm[:, h, :, 1, :], sm[:, h, :, 1, :],
                                             down[par][:, :, h].unsqueeze(2).to_broadcast([P, T, W1]), ALU.mult)
                ins.then_inc(downs, 1)
                pool.wait_ge(downs, b + 1)
                both = sm[:, :, :, :, :].rearrange("p h t k c -> p (h t) k c")
                pool.tensor_tensor(both[:, :, 0, :], both[:, :, 0, :], both[:, :, 1, :], ALU.add).then_inc(totals, 1)

            def stage(b, par, first, more):
                if more:
                    nm.pool_rstd(pool, b + 1)
                if not first:
                    combine(b - 1, 1 - par)
                if more:
                    prepare_parts(b + 1, 1 - par)

            walk(pool, prepare, stage, lambda: combine(B - 1, 1))

        @block.tensor
        def _(pe):
            pe.sem_inc(acc_summed, 8)
            pe.wait_ge(loaded, 16 * layer)

            def turn(n, par):
                pe.wait_ge(row_ready, n + 1)
                nm.pe_turn(pe, n, par)

            def values(n, par):
                pe.wait_ge(nm.h_t_ready, nm.upto(n))
                project_nodes(pe, aux_t, c.h_t, wv[:, :]).then_inc(v_projected, 1)

            def columns(n, par):
                pe.wait_ge(wh_ready, n + 1)
                for t in range(T):
                    ins = pe.matmul(aux[:, t * 2 * H:(t + 1) * 2 * H], c.h_t[:, t * P:(t + 1) * P],
                                    wa[:, :, :].rearrange("p k h -> p (k h)"), start=True, stop=True)
                ins.then_inc(sd_projected, 1)

            def rows(n, par):
                pe.wait_ge(sd_ready, n + 1)
                for i in range(2):
                    ins = pe.matmul(aux[0:H, i * HALF:(i + 1) * HALF], wa[:, 0, :],
                                    c.h_t[:, i * HALF:(i + 1) * HALF], start=True, stop=True)
                ins.then_inc(row_projected, 1)

            def prepare(n, par):
                for step in (turn, values, columns, rows):
                    step(n, par)

            if H == 4:
                table = {1: [turn], 2: [values], 3: [columns], 4: [rows]}
            else:
                table = {1: [turn], 2: [values], 3: [columns], 5: [rows]}

            def bases(b, par):
                for it in range(T):
                    if it >= 2:
                        pe.wait_ge(base_ready, T * b + it - 1)
                    for jt in range(T):
                        ins = pe.matmul(post[:, it % 2, 0:H * 3 * W1].rearrange("p (h k c) -> p h k c", h=H, k=3),
                                        c.edge[:, jt, it * P:(it + 1) * P], parts[par][:, jt, :, :, 1, :],
                                        start=(jt == 0), stop=(jt == T - 1))
                    ins.then_inc(base_summed, 1)

            def head(b, par, h, its):
                if its[0] == 0:
                    pe.wait_ge(g_ready, T * (H * b + h) + 3 * T)
                for it in its:
                    if it % 2 == 0:
                        pe.wait_ge(acc_read, 4 * (H * b + h) + it // 2 + 1)
                    o = (it % 2) * NS
                    for jt in range(T):
                        ins = pe.matmul(acc[:, it // 2, o:o + NS], g[h % 2][:, jt, it * P:(it + 1) * P],
                                        parts[par][:, jt, h, :, :, :].rearrange("p k a c -> p (k a c)"),
                                        start=(jt == 0), stop=(jt == T - 1))
                    if it % 2 == 1:
                        ins.then_inc(acc_summed, 1)

            def out_turn(b):
                pe.wait_ge(out_ready, b + 1)
                for t in range(T):
                    ins = pe.transpose(post_t[:, t, :], out[:, t, :], c.ident[:, :])
                ins.then_inc(out_turned, 1)

            def out_project(b):
                pe.wait_ge(out_t_ready, b + 1)
                project_nodes(pe, post_t, out_t, w_out[:, :]).then_inc(out_projected, 1)

            def stage(b, par, first, more):
                for h in range(H):
                    if h == 0:
                        pe.wait_ge(parts_ready, b + 1)
                    head(b, par, h, range(T // 2))
                    if more and H == 4:
                        pieces(table, 2 * h + 1, b + 1, 1 - par)
                    head(b, par, h, range(T // 2, T))
                    if H == 8 and h == 2:
                        bases(b, par)
                    if more:
                        pieces(table, 2 * h + 2 if H == 4 else h + 1, b + 1, 1 - par)
                    if H == 4 and h == 2:
                        bases(b, par)
                    if layer == 2 and not first:
                        if h == 3:
                            pe.wait_ge(base_ready, T * b + T)
                            out_turn(b - 1)
                        elif h == 4:
                            out_project(b - 1)

            def tail():
                if layer == 2:
                    out_turn(B - 1)
                    out_project(B - 1)

            walk(pe, prepare, stage, tail)

        @block.scalar
        def _(act):
            act.sem_inc(row_ready, 1)

            def copy(out_ap, in_ap, done):
                act.activation(out_ap, in_ap, ACT.Copy).then_inc(done, 1)

            def h(n, par):
                nm.act_h(act, n, par)

            def h_t(n, par):
                nm.act_h_t(act, n)

            def wh_out(n, par):
                act.wait_ge(v_projected, n + 1)
                copy(wh[:, :, :, :].rearrange("p t h d -> p (t h d)"), aux[:, :], wh_ready)

            def row_out(n, par):
                act.wait_ge(row_projected, n + 1)
                act.wait_ge(row_stored, 16 * n + 16)
                copy(s_row[:, :], aux[0:H, :], row_ready)

            def exps(n, par):
                act.wait_ge(z_parts, n + 1)
                act.activation(up[par][:, :, :], z_up[:, :, :], ACT.Exp)
                act.activation(down[par][:, :, :], z_down[:, :, :], ACT.Exp)
                prior = {"bias": c.prior[:, 0:1]} if layer == 2 else {}
                act.activation(keyf[:, :, :, 0], dz[:, :, :], ACT.Exp, **prior)
                act.activation(keyf[:, :, :, 1], dz[:, :, :], ACT.Exp, scale=0.2, **prior).then_inc(factors, 1)

            def hi(n, par):
                act.wait_ge(vals_ready, n + 1)
                copy(part(par, 0), all_vals(), hi_ready)

            def mid(n, par):
                act.wait_ge(rest1, n + 1)
                copy(part(par, 1), all_vals(), mid_ready)

            def prepare(n, par):
                for step in (h, h_t, wh_out, row_out, exps, hi, mid):
                    step(n, par)

            if H == 4:
                table = {1: [h], 2: [h_t], 3: [wh_out], 5: [row_out, exps], 6: [hi], 7: [mid]}
            else:
                table = {1: [h], 2: [h_t], 3: [wh_out], 6: [row_out, exps, hi], 7: [mid]}

            def compare(b, par, h, jt):
                x = T * (H * b + h) + 2 * T
                act.wait_ge(g_ready, x + OWN + jt - RING + 1 if jt >= RING else x - T + OWN + SC + jt - RING + 1)
                act.activation(steep[:, (SC * h + jt) % RING, :], s_all[:, h % 2, :], ACT.Relu,
                               bias=steep_d[par][:, jt, h:h + 1], scale=STEEP).then_inc(steep_ready, 1)

            def neg_exp(b):
                act.wait_ge(neg_ready, b + 1)
                act.activation(neg[:, :, :], neg[:, :, :], ACT.Exp).then_inc(exp_ready, 1)

            def out_t_copy(b):
                act.wait_ge(out_turned, b + 1)
                copy(out_t[:, :], post[:, :, :].rearrange("p a n -> p (a n)"), out_t_ready)

            def stage(b, par, first, more):
                for h in range(H):
                    act.wait_ge(s_loaded[h % 2], 16 * (H // 2) * b + 16 * (h // 2) + 16)
                    for jt in range(SC):
                        compare(b, par, h, jt)
                        if more and H == 4 and jt == SC // 2 - 1:
                            pieces(table, 2 * h, b + 1, 1 - par)
                    if more:
                        pieces(table, 2 * h + 1 if H == 4 else h, b + 1, 1 - par)
                    if not first:
                        if layer == 1 and h == 3:
                            neg_exp(b - 1)
                        elif layer == 2 and h == 4:
                            out_t_copy(b - 1)

            walk(act, prepare, stage, lambda: neg_exp(B - 1) if layer == 1 else out_t_copy(B - 1))

        @block.vector
        def _(dve):
            dve.sem_inc(g_ready, 2 * T)
            dve.sem_inc(acc_read, 4)

            def stats(n, par):
                nm.dve_stats(dve, n)
                nm.dve_moments(dve, n)

            def sd_out(n, par):
                dve.wait_ge(sd_projected, n + 1)
                dve.tensor_copy(sd[:, :, :, :].rearrange("p t k h -> p (t k h)"), aux[:, 0:T * 2 * H]).then_inc(sd_ready, 1)
                dve.wait_ge(sd_ready, n + 1)
                dve.tensor_reduce(top_part[:, :], sd[:, :, 1, :].rearrange("p t h -> p h t"), AX.X,
                                  ALU.max).then_inc(top_partial, 1)

            def zs(n, par):
                dve.wait_ge(top_ready, n + 1)
                all_top = top[:, :].unsqueeze(1).to_broadcast([P, T, H])
                dve.tensor_tensor(z[:, :, :], sd[:, :, 0, :], all_top, ALU.add)
                dve.tensor_tensor(dz[:, :, :], sd[:, :, 1, :], all_top, ALU.subtract).then_inc(z_ready, 1)
                dve.wait_ge(z_ready, n + 1)
                dve.tensor_scalar(z_up[:, :, :], z[:, :, :], 0.8, 0.0, ALU.mult, ALU.min)
                dve.tensor_scalar(z_down[:, :, :], z[:, :, :], -0.8, 0.0, ALU.mult, ALU.min)
                dve.tensor_scalar(steep_d[par][:, :, :], sd[:, :, 1, :], STEEP, None, ALU.mult)
                dve.tensor_scalar(minus_d[par][:, :, :], sd[:, :, 1, :], -1.0, None, ALU.mult).then_inc(z_parts, 1)

            def weigh(n, par):
                dve.wait_ge(factors, n + 1)
                dve.wait_ge(wh_ready, n + 1)
                to = vals[:, :, :, :, :].rearrange("p t h k c -> p (t h) k c")
                f = keyf[:, :, :, :].rearrange("p t h k -> p (t h) k")
                for k in range(2):
                    dve.tensor_tensor(to[:, :, k, 0:DH], wh[:, :, :, :].rearrange("p t h d -> p (t h) d"),
                                      f[:, :, k:k + 1].to_broadcast([P, T * H, DH]), ALU.mult)
                dve.tensor_copy(to[:, :, :, DH], f).then_inc(vals_ready, 1)

            def prepare(n, par):
                for step in (stats, sd_out, zs, weigh):
                    step(n, par)
                if layer == 1:
                    dve.wait_ge(adj_loaded, 16 * T)
                    for i in range(2):
                        ins = dve.tensor_scalar(c.edge[:, 4 * i:4 * i + 4, :], adj_in[i], 0, None, ALU.is_gt)
                    ins.then_inc(edge_ready, 1)
                    dve.wait_ge(edge_ready, 1)

            if H == 4:
                table = {0: [stats], 4: [sd_out], 5: [zs, weigh]}
            else:
                table = {0: [stats], 4: [sd_out], 5: [zs], 6: [weigh]}

            def read_sums(b, par, h, pair):
                dve.wait_ge(acc_summed, 4 * (H * b + h) + pair + 9)
                dve.tensor_reduce(sums[par][:, h, 2 * pair:2 * pair + 2, :, :].rearrange("p i k c -> p i (k c)"),
                                  acc[:, pair, 0:2 * NS].rearrange("p (i k c) -> p i c k", i=2, k=3),
                                  AX.X, ALU.add).then_inc(acc_read, 1)

            def read_base(b, par, it):
                dve.wait_ge(base_summed, T * b + it + 1)
                dve.tensor_reduce(base[par][:, it, :, :],
                                  post[:, it % 2, 0:H * 3 * W1].rearrange("p (h k c) -> p h c k", h=H, k=3),
                                  AX.X, ALU.add).then_inc(base_ready, 1)

            def post_a(b, par):
                dve.wait_ge(totals, b + 1)
                dve.reciprocal(inv[:, :, :], sums[par][:, :, :, 0, DH]).then_inc(inverted, 1)
                dve.wait_ge(inverted, b + 1)
                dve.tensor_tensor(out[:, :, :].rearrange("p t (h d) -> p h t d", h=H), sums[par][:, :, :, 0, 0:DH],
                                  inv[:, :, :].unsqueeze(3).to_broadcast([P, H, T, DH]), ALU.mult).then_inc(out_ready, 1)
                if layer == 1:
                    dve.wait_ge(out_ready, b + 1)
                    dve.tensor_scalar(neg[:, :, :], out[:, :, :], 0.0, None, ALU.min).then_inc(neg_ready, 1)

            def post_b(b):
                xb = c.x[:, b, :, :]
                if layer == 1:
                    dve.scalar_tensor_tensor(out=xb, in0=out[:, :, :], scalar=0.0, in1=xb, op0=ALU.max,
                                             op1=ALU.add).then_inc(x_relu, 1)
                    dve.wait_ge(x_relu, b + 1)
                    dve.wait_ge(exp_ready, b + 1)
                    dve.scalar_tensor_tensor(out=xb, in0=neg[:, :, :], scalar=-1.0, in1=xb, op0=ALU.add,
                                             op1=ALU.add).then_inc(x_updated, 1)
                else:
                    dve.wait_ge(out_projected, b + 1)
                    dve.tensor_tensor(xb, xb, post_t, ALU.add).then_inc(x_updated, 1)
                dve.wait_ge(x_updated, b + 1)

            def make_g(b, par, h, step):
                x = H * b + h
                if step < OWN:
                    jt = SC + step
                    if step == 0:
                        dve.wait_ge(s_loaded[h % 2], 16 * (H // 2) * b + 16 * (h // 2) + 16)
                        dve.wait_ge(acc_summed, 4 * x + 4)
                    dve.scalar_tensor_tensor(out=g[h % 2][:, jt, :], in0=s_all[:, h % 2, :],
                                             scalar=minus_d[par][:, jt, h:h + 1], in1=c.edge[:, jt, :],
                                             op0=ALU.is_gt, op1=ALU.mult).then_inc(g_ready, 1)
                else:
                    jt = step - OWN
                    dve.wait_ge(steep_ready, SC * x + jt + 1)
                    dve.tensor_tensor(g[h % 2][:, jt, :], steep[:, (SC * h + jt) % RING, :], c.edge[:, jt, :],
                                      ALU.min).then_inc(g_ready, 1)

            def stage(b, par, first, more):
                for h in range(H):
                    for step in range(T):
                        make_g(b, par, h, step)
                        if step in (2, 4, 6, 7):
                            pair = (2, 4, 6, 7).index(step)
                            if h > 0:
                                read_sums(b, par, h - 1, pair)
                            elif not first:
                                read_sums(b - 1, 1 - par, H - 1, pair)
                        if h == 3:
                            read_base(b, par, step)
                        if more and H == 4 and step == 3:
                            pieces(table, 2 * h, b + 1, 1 - par)
                    if more:
                        pieces(table, 2 * h + 1 if H == 4 else h, b + 1, 1 - par)
                    if not first:
                        if h == 2:
                            post_a(b - 1, 1 - par)
                        elif h == (3 if H == 4 else 6):
                            post_b(b - 1)

            def tail():
                for pair in range(4):
                    read_sums(B - 1, 1, H - 1, pair)
                post_a(B - 1, 1)
                post_b(B - 1)

            walk(dve, prepare, stage, tail)
    return sems


def additive_layer_wide(c, layer, w, sems):
    nc = c.nc
    H = HEADS[layer]
    DH = F // H
    STEPS = 5
    L = f"w{layer}"
    free = iter(sems)
    sem = lambda: next(free)
    with ExitStack() as ctx:
        sb = lambda name, shape, dt=F32: c.sb(name + L, shape, dt, ctx)
        wv, w_out, out_t = sb("wv", [P, F]), sb("w_out", [P, F]), sb("out_t", [P, N])
        adj_in = sb("adj_in", [P, 2, N], I32)
        bias = sb("bias", [P, T, N], BF16)
        wh, sd = sb("wh", [P, T, H, DH]), sb("sd", [P, T, 2, H])
        d_row, d_all = sb("d_row", [H, N]), sb("d_all", [P, N])
        z, zt = sb("z", [P, N]), sb("zt", [P, T, P])
        top, leaky_top, shift = sb("top", [P, 1]), sb("leaky_top", [P, 1]), sb("shift", [P, 1])
        total, inv = sb("total", [P, 1]), sb("inv", [P, 1])
        out, neg = sb("out", [P, T, H, DH]), sb("neg", [P, T, F])
        t_ps = c.ps("t_ps" + L, [P, N], ctx)
        o_ps = c.ps("o_ps" + L, [P, HALF], ctx)
        aux = c.ps("aux" + L, [P, N], ctx)
        aux_t = aux[:, :].rearrange("p (t f) -> p t f", t=T)
        d_dram = nc.dram_tensor("d_rows" + L, (H, N), F32, kind="Internal").ap()
        out_f = out[:, :, :, :].rearrange("p t h d -> p t (h d)")
        nm = Norm(c, layer, aux)
        loaded, adj_loaded, adj_used = sem(), sem(), sem()
        v_projected, wh_ready, sd_projected, sd_ready, row_projected, row_ready, row_stored, d_loaded = (
            sem() for _ in range(8))
        shaped, exp_done, turned, copied, pv_done, inverted, out_done = (sem() for _ in range(7))
        end_a, end_b, end_c, x_updated = (sem() for _ in range(4))
        block = ctx.enter_context(nc.Block())

        def graphs(eng, graph, tile):
            with eng.Fori(0, B) as b:
                graph(b, False)
                with eng.Fori(0, H) as h:
                    n = H * b + h
                    for t in range(T):
                        tile(T * n + t, n, h, t)
                graph(b, True)

        @block.sync
        def _(sp):
            sp.sem_inc(row_stored, 16)
            sp.dma_start(wv[:, :], w["wv"]).then_inc(loaded, 16)
            if layer == 2:
                sp.dma_start(w_out[:, :], w["w_out_t"]).then_inc(loaded, 16)
            for i in range(2 * T):
                src = (w["adj"], w["adj_t"])[i // T]
                if i < (2 * T if layer == 1 else T):
                    if i >= 1:
                        sp.wait_ge(adj_used, i)
                    sp.dma_start(adj_in[:, i % 2, :], src[(i % T) * P:(i % T + 1) * P, :]).then_inc(adj_loaded, 16)

            def graph(b, end):
                if not end:
                    sp.wait_ge(row_ready, b + 1)
                    sp.dma_start(d_dram, d_row[:, :]).then_inc(row_stored, 16)
                    wait_apart(c, sp, row_stored, 16 * b + 32)

            def tile(m, n, h, t):
                if t == 0:
                    wait_apart(c, sp, out_done, m + 1)
                    sp.dma_start(d_all[:, :], d_dram[bass.ds(h, 1), :].to_broadcast([P, N])).then_inc(d_loaded, 16)

            graphs(sp, graph, tile)

        @block.gpsimd
        def _(pool):
            with pool.Fori(0, B) as b:
                nm.pool_rstd(pool, b)

        @block.tensor
        def _(pe):
            pe.sem_inc(turned, 1)
            pe.sem_inc(pv_done, 1)
            pe.wait_ge(loaded, 16 * layer)

            def graph(b, end):
                if not end:
                    pe.wait_ge(x_updated, b + 1)
                    nm.pe_turn(pe, b, 0)
                    pe.wait_ge(nm.h_t_ready, nm.upto(b))
                    project_nodes(pe, aux_t, c.h_t, wv[:, :]).then_inc(v_projected, 1)
                    pe.wait_ge(wh_ready, b + 1)
                    for t in range(T):
                        ins = pe.matmul(aux[:, t * 2 * H:(t + 1) * 2 * H], c.h_t[:, t * P:(t + 1) * P],
                                        c.wa[layer][:, :, :].rearrange("p k h -> p (k h)"), start=True, stop=True)
                    ins.then_inc(sd_projected, 1)
                    pe.wait_ge(sd_ready, b + 1)
                    for i in range(2):
                        ins = pe.matmul(aux[0:H, i * HALF:(i + 1) * HALF], c.wa[layer][:, 1, :],
                                        c.h_t[:, i * HALF:(i + 1) * HALF], start=True, stop=True)
                    ins.then_inc(row_projected, 1)
                elif layer == 2:
                    pe.wait_ge(out_done, (b + 1) * (H * T) + 1)
                    for t in range(T):
                        ins = pe.transpose(aux_t[:, t, :], out_f[:, t, :], c.ident[:, :])
                    ins.then_inc(end_a, 1)
                    pe.wait_ge(end_b, b + 1)
                    project_nodes(pe, aux_t, out_t, w_out[:, :]).then_inc(end_c, 1)

            def tile(m, n, h, t):
                pe.wait_ge(exp_done, m + 1)
                pe.wait_ge(copied, m + 1)
                for k in range(T):
                    ins = pe.transpose(t_ps[:, k * P:(k + 1) * P], z[:, k * P:(k + 1) * P], c.ident[:, :])
                ins.then_inc(turned, 1)
                pe.wait_ge(copied, m + 2)
                pe.wait_ge(out_done, m + 1)
                for k in range(T):
                    ins = pe.matmul(o_ps[:, 0:F], zt[:, k, :], wh[:, k, :, :].rearrange("p h d -> p (h d)"),
                                    start=(k == 0), stop=(k == T - 1))
                ins.then_inc(pv_done, 1)

            graphs(pe, graph, tile)

        @block.scalar
        def _(act):
            act.sem_inc(copied, 1)

            def graph(b, end):
                if not end:
                    nm.act_h(act, b, 0)
                    nm.act_h_t(act, b)
                    act.wait_ge(v_projected, b + 1)
                    act.activation(wh[:, :, :, :].rearrange("p t h d -> p (t h d)"), aux[:, :],
                                   ACT.Copy).then_inc(wh_ready, 1)
                    act.wait_ge(row_projected, b + 1)
                    act.wait_ge(row_stored, 16 * b + 16)
                    act.activation(d_row[:, :], aux[0:H, :], ACT.Copy).then_inc(row_ready, 1)
                elif layer == 1:
                    act.wait_ge(end_a, b + 1)
                    act.activation(neg[:, :, :], neg[:, :, :], ACT.Exp).then_inc(end_b, 1)
                else:
                    act.wait_ge(end_a, b + 1)
                    act.activation(out_t[:, :], aux[:, :], ACT.Copy).then_inc(end_b, 1)

            def tile(m, n, h, t):
                act.wait_ge(shaped, STEPS * m + STEPS)
                act.activation(z[:, :], z[:, :], ACT.Exp, bias=shift[:, 0:1],
                               accum_out=total[:, 0:1]).then_inc(exp_done, 1)
                act.wait_ge(turned, m + 2)
                act.wait_ge(pv_done, m + 1)
                act.activation(zt[:, :, :].rearrange("p t n -> p (t n)"), t_ps[:, :], ACT.Copy).then_inc(copied, 1)

            graphs(act, graph, tile)

        @block.vector
        def _(dve):
            dve.sem_inc(out_done, 1)
            dve.sem_inc(x_updated, 1)
            for i in range(2 * T if layer == 1 else T):
                dve.wait_ge(adj_loaded, 16 * (i + 1))
                a = adj_in[:, i % 2, :]
                if i < T:
                    dve.tensor_scalar(bias[:, i, :], a, 0, NEG, ALU.is_le, ALU.mult).then_inc(adj_used, 1)
                else:
                    dve.tensor_scalar(c.edge[:, i - T, :], a, 0, None, ALU.is_gt).then_inc(adj_used, 1)
            dve.wait_ge(adj_used, T * (2 if layer == 1 else 1))

            def graph(b, end):
                xb = c.x[:, b, :, :]
                if not end:
                    nm.dve_stats(dve, b)
                    nm.dve_moments(dve, b)
                    dve.wait_ge(sd_projected, b + 1)
                    dve.tensor_copy(sd[:, :, :, :].rearrange("p t k h -> p (t k h)"),
                                    aux[:, 0:T * 2 * H]).then_inc(sd_ready, 1)
                    wait_apart(c, dve, sd_ready, b + 1)
                    return
                if layer == 1:
                    dve.wait_ge(out_done, (b + 1) * (H * T) + 1)
                    dve.tensor_scalar(neg[:, :, :], out_f, 0.0, None, ALU.min).then_inc(end_a, 1)
                    dve.scalar_tensor_tensor(out=xb, in0=out_f, scalar=0.0, in1=xb, op0=ALU.max,
                                             op1=ALU.add).then_inc(end_c, 1)
                    dve.wait_ge(end_c, b + 1)
                    dve.wait_ge(end_b, b + 1)
                    dve.scalar_tensor_tensor(out=xb, in0=neg[:, :, :], scalar=-1.0, in1=xb, op0=ALU.add,
                                             op1=ALU.add).then_inc(x_updated, 1)
                else:
                    dve.wait_ge(end_c, b + 1)
                    dve.tensor_tensor(xb, xb, aux_t, ALU.add).then_inc(x_updated, 1)
                dve.wait_ge(x_updated, b + 2)

            def tile(m, n, h, t):
                if t == 0:
                    dve.wait_ge(d_loaded, 16 * n + 16)
                dve.wait_ge(turned, m + 1)
                dve.tensor_tensor(z[:, :], d_all[:, :], bias[:, t, :], ALU.add).then_inc(shaped, 1)
                dve.wait_ge(shaped, STEPS * m + 1)
                dve.tensor_reduce(top[:, :], z[:, :], AX.X, ALU.max).then_inc(shaped, 1)
                dve.wait_ge(shaped, STEPS * m + 2)
                s = sd[:, t, 0, bass.ds(h, 1)]
                dve.tensor_scalar(z[:, :], z[:, :], s, None, ALU.add)
                dve.tensor_scalar(top[:, :], top[:, :], s, None, ALU.add).then_inc(shaped, 1)
                dve.wait_ge(shaped, STEPS * m + 3)
                dve.scalar_tensor_tensor(out=z[:, :], in0=z[:, :], scalar=0.2, in1=z[:, :], op0=ALU.mult, op1=ALU.max)
                dve.scalar_tensor_tensor(out=leaky_top[:, :], in0=top[:, :], scalar=0.2, in1=top[:, :], op0=ALU.mult,
                                         op1=ALU.max).then_inc(shaped, 1)
                dve.wait_ge(shaped, STEPS * m + 4)
                if layer == 2:
                    dve.tensor_scalar(shift[:, :], leaky_top[:, :], -1.0, c.prior[:, 0:1], ALU.mult,
                                      ALU.add).then_inc(shaped, 1)
                else:
                    dve.tensor_scalar(shift[:, :], leaky_top[:, :], -1.0, None, ALU.mult).then_inc(shaped, 1)
                dve.wait_ge(pv_done, m + 2)
                dve.reciprocal(inv[:, :], total[:, :]).then_inc(inverted, 1)
                dve.wait_ge(inverted, m + 1)
                dve.tensor_scalar(out[:, t, bass.ds(h, 1), :], o_ps[:, 0:F].rearrange("p (h d) -> p h d", h=H)[:, bass.ds(h, 1), :],
                                  inv[:, 0:1], None, ALU.mult).then_inc(out_done, 1)

            graphs(dve, graph, tile)


def layer3(c, x_out, adj, w):
    nc = c.nc
    KEEP = 4
    with ExitStack() as ctx:
        sb = lambda name, shape, dt=F32: c.sb(name, shape, dt, ctx)
        adj_in = sb("adj_in3", [P, 2, N], I32)
        bias = sb("bias3", [P, T, N], BF16)
        w1, w2, w3 = (sb(k, [P, F]) for k in ("w1", "w2", "w3"))
        q = [sb(f"q3_{i}", [P, N]) for i in range(2)]
        k = [sb(f"k3_{i}", [P, N]) for i in range(2)]
        v = [sb(f"v3_{i}", [P, T, F]) for i in range(2)]
        z = sb("z3", [P, 2, N])
        zt = sb("zt3", [P, T, P])
        top, minus, shift = sb("top3", [P, 2]), sb("minus3", [P, 2]), sb("shift3", [P, 2])
        total, inv = sb("total3", [P, KEEP]), sb("inv3", [P, KEEP])
        res = sb("res3", [P, F])
        s_ps = c.ps("s3_ps", [P, N], ctx)
        t_ps = c.ps("t3_ps", [P, 2, HALF], ctx)
        o_ps = c.ps("o3_ps", [P, 2, HALF], ctx)
        aux = c.ps("aux3", [P, N], ctx)
        aux_t = aux[:, :].rearrange("p (t f) -> p t f", t=T)

        sem = lambda name: c.sem(name + "3")
        nm = Norm(c, 3, aux)
        loaded, adj_loaded, adj_used = sem("weights"), [sem("adj_a"), sem("adj_b")], sem("adj_used")
        q_projected, q_ready, k_projected, k_ready, v_projected, v_ready = (
            sem(s) for s in ("q_projected", "q_ready", "k_projected", "k_ready", "v_projected", "v_ready"))
        s_ready, biased, minus_ready, shift_ready, leaky = (
            sem(s) for s in ("s_ready", "biased", "minus_ready", "shift_ready", "leaky"))
        exp_done, turned, zt_low, zt_high, o_ready = (
            sem(s) for s in ("exp_done", "turned", "zt_low", "zt_high", "o_ready"))
        inverted, res_ready, x_updated, stored = (sem(s) for s in ("inverted", "res_ready", "x_updated", "stored"))
        block = ctx.enter_context(nc.Block())

        @block.sync
        def _(sp):
            for dst, name in ((w1, "w1"), (w2, "w2"), (w3, "w3")):
                sp.dma_start(dst[:, :], w[name]).then_inc(loaded, 16)
            for t in range(T):
                if t >= 2:
                    sp.wait_ge(adj_used, t - 1)
                sp.dma_start(adj_in[:, t % 2, :], adj[t * P:(t + 1) * P, :]).then_inc(adj_loaded[t % 2], 16)

            def store(b):
                wait_apart(c, sp, x_updated, T * (b + 1))
                sp.dma_start(x_out[b].rearrange("(t p) f -> p t f", p=P), c.x[:, b, :, :]).then_inc(stored, 16)

            def stage(b, par, first, more):
                if not first:
                    store(b - 1)

            walk(sp, lambda n, par: None, stage, lambda: store(B - 1))
            sp.wait_ge(stored, 16 * B)

        @block.gpsimd
        def _(pool):
            def stage(b, par, first, more):
                if more:
                    nm.pool_rstd(pool, b + 1)

            walk(pool, lambda n, par: nm.pool_rstd(pool, n), stage)

        @block.tensor
        def _(pe):
            pe.wait_ge(loaded, 48)

            def turn(n, par):
                if not (isinstance(n, int) and n == 0):
                    pe.wait_ge(v_ready, n)
                nm.pe_turn(pe, n, par)

            def q_rows(n, par):
                pe.wait_ge(nm.h_t_ready, nm.upto(n))
                project_rows(pe, aux, w1[:, :], c.h_t).then_inc(q_projected, 1)

            def k_rows(n, par):
                pe.wait_ge(q_ready, n + 1)
                project_rows(pe, aux, w2[:, :], c.h_t).then_inc(k_projected, 1)

            def v_nodes(n, par):
                pe.wait_ge(k_ready, n + 1)
                project_nodes(pe, aux_t, c.h_t, w3[:, :]).then_inc(v_projected, 1)

            def prepare(n, par):
                for step in (turn, q_rows, k_rows, v_nodes):
                    step(n, par)

            table = {2: turn, 4: q_rows, 6: k_rows, 7: v_nodes}

            def scores(m, par, i):
                if not (isinstance(m, int) and m == 0):
                    pe.wait_ge(biased, m)
                for j in range(2):
                    ins = pe.matmul(s_ps[:, j * HALF:(j + 1) * HALF], q[par][:, i * P:(i + 1) * P],
                                    k[par][:, j * HALF:(j + 1) * HALF], start=True, stop=True)
                ins.then_inc(s_ready, 1)

            def turn_weights(m, i):
                pe.wait_ge(exp_done, m + 1)
                if not (isinstance(m, int) and m == 0):
                    pe.wait_ge(zt_low, m)
                    pe.wait_ge(zt_high, m)
                for t in range(T):
                    ins = pe.transpose(t_ps[:, t // 4, (t % 4) * P:(t % 4 + 1) * P], z[:, i % 2, t * P:(t + 1) * P],
                                       c.ident[:, :])
                ins.then_inc(turned, 1)

            def values(m, par, i):
                pe.wait_ge(zt_low, m + 1)
                pe.wait_ge(zt_high, m + 1)
                for t in range(T):
                    ins = pe.matmul(o_ps[:, i % 2, 0:F], zt[:, t, :], v[par][:, t, :], start=(t == 0), stop=(t == T - 1))
                ins.then_inc(o_ready, 1)

            def step(b, par, i, first):
                m = T * b + i
                if i < T:
                    scores(m, par, i)
                if not (first and i < 2):
                    values(m - 2, par if i >= 2 else 1 - par, i % 2)
                if not (first and i < 1) and i < T + 1:
                    turn_weights(m - 1, (i + 1) % 2)

            def stage(b, par, first, more):
                pe.wait_ge(q_ready, b + 1)
                pe.wait_ge(k_ready, b + 1)
                for i in range(T):
                    if i == 2:
                        pe.wait_ge(v_ready, b + 1)
                    step(b, par, i, first)
                    if more and i in table:
                        table[i](b + 1, 1 - par)

            def tail():
                step(B - 1, 1, T, False)
                step(B - 1, 1, T + 1, False)

            walk(pe, prepare, stage, tail)

        @block.scalar
        def _(act):
            def h(n, par):
                nm.act_h(act, n, par)

            def h_t(n, par):
                nm.act_h_t(act, n)

            def q_out(n, par):
                act.wait_ge(q_projected, n + 1)
                act.activation(q[par][:, :], aux[:, :], ACT.Copy).then_inc(q_ready, 1)

            def v_out(n, par):
                act.wait_ge(v_projected, n + 1)
                act.activation(v[par][:, :, :], aux_t, ACT.Copy).then_inc(v_ready, 1)

            def prepare(n, par):
                for step in (h, h_t, q_out, v_out):
                    step(n, par)

            table = {1: h, 3: h_t, 4: q_out, 7: v_out}

            def exps(m, i):
                act.wait_ge(leaky, m + 1)
                act.wait_ge(shift_ready, m + 1)
                tile = z[:, i % 2, :]
                act.activation(tile, tile, ACT.Exp, bias=shift[:, i % 2:i % 2 + 1],
                               accum_out=total[:, i % KEEP:i % KEEP + 1]).then_inc(exp_done, 1)

            def low_half(m):
                act.wait_ge(turned, m + 1)
                act.activation(zt[:, 0:4, :], t_ps[:, 0, :].rearrange("p (t n) -> p t n", t=4), ACT.Copy).then_inc(zt_low, 1)

            def step(b, i, first):
                m = T * b + i
                if i < T:
                    exps(m, i)
                if not (first and i < 1):
                    low_half(m - 1)

            def stage(b, par, first, more):
                for i in range(T):
                    step(b, i, first)
                    if more and i in table:
                        table[i](b + 1, 1 - par)

            walk(act, prepare, stage, lambda: step(B - 1, T, False))

        @block.vector
        def _(dve):
            def stats(n, par):
                nm.dve_stats(dve, n)
                nm.dve_moments(dve, n)

            def k_out(n, par):
                dve.wait_ge(k_projected, n + 1)
                dve.tensor_copy(k[par][:, :], aux[:, :]).then_inc(k_ready, 1)

            def prepare(n, par):
                for step in (stats, k_out):
                    step(n, par)
                for t in range(T):
                    dve.wait_ge(adj_loaded[t % 2], 16 * (t // 2 + 1))
                    dve.tensor_scalar(bias[:, t, :], adj_in[:, t % 2, :], 0, NEG, ALU.is_le,
                                      ALU.mult).then_inc(adj_used, 1)
                dve.wait_ge(adj_used, T)

            table = {0: stats, 6: k_out}

            def mask(m, i):
                a = i % 2
                wait_apart(c, dve, s_ready, m + 1)
                dve.tensor_tensor_reduce(z[:, a, :], s_ps[:, :], bias[:, i, :], 1.0, -3.0e38, ALU.add, ALU.max,
                                         top[:, a:a + 1]).then_inc(biased, 1)
                dve.wait_ge(biased, m + 1)
                dve.tensor_scalar(minus[:, a:a + 1], top[:, a:a + 1], -1.0, None, ALU.mult).then_inc(minus_ready, 1)
                dve.scalar_tensor_tensor(out=z[:, a, :], in0=z[:, a, :], scalar=0.2, in1=z[:, a, :], op0=ALU.mult,
                                         op1=ALU.max).then_inc(leaky, 1)
                dve.wait_ge(minus_ready, m + 1)
                dve.scalar_tensor_tensor(out=shift[:, a:a + 1], in0=top[:, a:a + 1], scalar=-0.2,
                                         in1=minus[:, a:a + 1], op0=ALU.mult, op1=ALU.min).then_inc(shift_ready, 1)

            def high_half(m):
                dve.wait_ge(turned, m + 1)
                dve.tensor_copy(zt[:, 4:8, :], t_ps[:, 1, :].rearrange("p (t n) -> p t n", t=4)).then_inc(zt_high, 1)

            def output(m, b, i):
                a = i % KEEP
                dve.reciprocal(inv[:, a:a + 1], total[:, a:a + 1]).then_inc(inverted, 1)
                dve.wait_ge(inverted, m + 1)
                dve.wait_ge(o_ready, m + 1)
                dve.tensor_scalar(res[:, :], o_ps[:, i % 2, 0:F], inv[:, a:a + 1], 0.0, ALU.mult,
                                  ALU.max).then_inc(res_ready, 1)
                dve.wait_ge(res_ready, m + 1)
                xt = c.x[:, b, i, :]
                dve.tensor_tensor(xt, xt, res[:, :], ALU.add).then_inc(x_updated, 1)

            def step(b, i, first):
                m = T * b + i
                if i < T:
                    mask(m, i)
                if not (first and i < 1) and i < T + 1:
                    high_half(m - 1)
                if not (first and i < 2):
                    output(m - 2, b if i >= 2 else b - 1, (i - 2) % T)

            def stage(b, par, first, more):
                for i in range(T):
                    step(b, i, first)
                    if more and i in table:
                        table[i](b + 1, 1 - par)

            def tail():
                step(B - 1, T, False)
                step(B - 1, T + 1, False)

            walk(dve, prepare, stage, tail)


def build(nc, a, out, layers=(0, 1, 2, 3)):
    with ExitStack() as ctx:
        c = Core(nc, ctx)
        if 0 in layers:
            layer0(c, a["x"], a["adj_t"], a)
        c.edge = c.sb("edge", [P, T, N], BF16)
        for layer in HEADS:
            if layer in layers:
                w = {"wv": a[f"w_{layer}"], "w_out_t": a["w_out_t"], "adj": a["adj"], "adj_t": a["adj_t"]}
                wide = nc.values_load(c.wide[0:1, layer - 1:layer], min_val=0, max_val=1)
                with nc.If(wide == 0):
                    sems = additive_layer(c, layer, w)
                with nc.Else():
                    additive_layer_wide(c, layer, w, sems)
        if 3 in layers:
            layer3(c, out, a["adj"], a)
            return
        done = c.sem("out_stored")
        with nc.Block() as block:
            @block.sync
            def _(sp):
                for b in range(B):
                    sp.dma_start(out[b].rearrange("(t p) f -> p t f", p=P), c.x[:, b, :, :]).then_inc(done, 16)
                sp.wait_ge(done, 16 * B)


def layouts(x, adj, L0_gnn_Wq, L0_gnn_bq, L0_gnn_Wk, L0_gnn_bk, L0_gnn_Wv, L0_gnn_bv, L0_gnn_Wo, L0_gnn_bo,
            L0_gnn_gamma, L0_gnn_beta, L1_gnn_W, L1_gnn_a, L2_gnn_W, L2_gnn_a_src, L2_gnn_a_dst,
            L2_gnn_beta_tilde, L2_gnn_W_out, L3_gnn_W1, L3_gnn_W2, L3_gnn_W3):
    import numpy as _np

    k, m, j = _np.ogrid[0:P, 0:P, 0:T]
    return {
        "pick": _np.ascontiguousarray(_np.broadcast_to(m[:, 0:32].transpose(0, 2, 1) % T == j.transpose(0, 2, 1),
                                                       (P, T, 32)), _np.float32),
        "spread": _np.ascontiguousarray((k == 32 * (m // 32) + j).transpose(0, 2, 1), _np.float32),
        "x": x, "adj": adj, "adj_t": adj.T,
        "wq_t": L0_gnn_Wq.T, "wk_t": L0_gnn_Wk.T, "wv_t": L0_gnn_Wv.T, "wo_t": L0_gnn_Wo.T,
        "bq": L0_gnn_bq.reshape(F, 1), "bk": L0_gnn_bk.reshape(F, 1), "bv": L0_gnn_bv, "bo": L0_gnn_bo,
        "gamma": L0_gnn_gamma, "beta": L0_gnn_beta,
        "w_1": L1_gnn_W.transpose(1, 0, 2).reshape(F, F),
        "a_1": L1_gnn_a.reshape(4, 2, F // 4).transpose(1, 0, 2).reshape(2 * F),
        "w_2": L2_gnn_W.transpose(1, 0, 2).reshape(F, F),
        "a_2": _np.stack([L2_gnn_a_src, L2_gnn_a_dst]).reshape(2 * F),
        "beta_tilde": L2_gnn_beta_tilde.reshape(1), "w_out_t": L2_gnn_W_out.T,
        "w1": L3_gnn_W1, "w2": L3_gnn_W2, "w3": L3_gnn_W3,
    }


def kernel(**inputs):
    import numpy as _np
    import concourse.bacc as _bacc
    from concourse import mybir as _mybir
    from concourse.bass_utils import run_bass_kernel_spmd as _run

    nc = _bacc.Bacc("TRN2", target_bir_lowering=False, num_devices=1)
    arrays = {f"in_{k}": _np.ascontiguousarray(v) for k, v in layouts(**inputs).items()}
    args = {k[3:]: nc.dram_tensor(k, v.shape, _mybir.dt.from_np(v.dtype), kind="ExternalInput").ap()
            for k, v in arrays.items()}
    out = nc.dram_tensor("out_x", (B, N, F), F32, kind="ExternalOutput").ap()
    build(nc, args, out)
    return _run(nc, [arrays], core_ids=[0]).results[0]["out_x"]
```
